# Optimizing a Trainium2 kernel written in Bass

```python
import numpy as np
import jax
import jax.numpy as jnp

def _softmax(x, axis=-1):
    return jax.nn.softmax(x, axis=axis)

def _gelu(x):
    return jax.nn.gelu(x, approximate=True)

def _silu(x):
    return jax.nn.silu(x)

def _sigmoid(x):
    return jax.nn.sigmoid(x)

def _layernorm(x, axis=-1, eps=1e-05):
    m = jnp.mean(x, axis=axis, keepdims=True)
    v = jnp.var(x, axis=axis, keepdims=True)
    return (x - m) / jnp.sqrt(v + eps)

def _scatter_add(tgt, idx, src, axis=0):
    return tgt.at[idx].add(src)

def _segment_sum(src, seg, n):
    return jax.ops.segment_sum(src, seg, n)
kernel_name = 'mk_seq_preln_d1_jaxref_r8_9f2772'

def setup_inputs(seed: int=0):
    np.random.seed(seed)
    _w = jnp.asarray

    def _L0_attn_setup():
        import jax, jax.numpy as jnp
        import numpy as np
        NUM_HEADS = 1
        LN_EPS = 1e-05
        key = jax.random.key(seed)
        ks = jax.random.split(key, 4)
        B, L, D = (8, 512, 128)
        x = jax.random.normal(ks[0], (B, L, D), dtype=jnp.float32)
        qkv_w = jax.random.normal(ks[1], (3 * D, D), dtype=jnp.float32) * np.float32(np.sqrt(1.0 / D))
        qkv_b = jnp.zeros((3 * D,), dtype=jnp.float32)
        proj_w = jax.random.normal(ks[2], (D, D), dtype=jnp.float32) * np.float32(np.sqrt(1.0 / D))
        proj_b = jnp.zeros((D,), dtype=jnp.float32)
        return {'x': x, 'norm_w': jnp.ones((D,), dtype=jnp.float32), 'norm_b': jnp.zeros((D,), dtype=jnp.float32), 'qkv_w': qkv_w, 'qkv_b': qkv_b, 'proj_w': proj_w, 'proj_b': proj_b}
    _L0_attn_in = _L0_attn_setup()

    def _L0_ffn_setup():
        import jax, jax.numpy as jnp
        import numpy as np
        E, D, F = (8, 128, 512)
        B, S = (4, 256)

        def _layernorm(x, g, b, eps=1e-05):
            mu = jnp.mean(x, axis=-1, keepdims=True)
            var = jnp.var(x, axis=-1, keepdims=True)
            return (x - mu) * jax.lax.rsqrt(var + eps) * g + b
        key = jax.random.key(seed)
        ks = jax.random.split(key, 5)
        return {'input_features': jax.random.normal(ks[0], (B, S, D), jnp.float32), 'centroids': jax.random.normal(ks[1], (E, D), jnp.float32) * 0.1, 'ln_g': jnp.ones((E, D), jnp.float32), 'ln_b': jnp.zeros((E, D), jnp.float32), 'w1': jax.random.normal(ks[2], (E, F, D), jnp.float32) * (1.0 / np.sqrt(D).astype(np.float32)), 'b1': jnp.zeros((E, F), jnp.float32), 'w2': jax.random.normal(ks[3], (E, D, F), jnp.float32) * (1.0 / np.sqrt(F).astype(np.float32)), 'b2': jnp.zeros((E, D), jnp.float32)}
    _L0_ffn_in = _L0_ffn_setup()
    _d = {'L0_attn_x': _L0_attn_in['x'], 'L0_attn_norm_w': _L0_attn_in['norm_w'], 'L0_attn_norm_b': _L0_attn_in['norm_b'], 'L0_attn_qkv_w': _L0_attn_in['qkv_w'], 'L0_attn_qkv_b': _L0_attn_in['qkv_b'], 'L0_attn_proj_w': _L0_attn_in['proj_w'], 'L0_attn_proj_b': _L0_attn_in['proj_b'], 'L0_ffn_centroids': _L0_ffn_in['centroids'], 'L0_ffn_ln_g': _L0_ffn_in['ln_g'], 'L0_ffn_ln_b': _L0_ffn_in['ln_b'], 'L0_ffn_w1': _L0_ffn_in['w1'], 'L0_ffn_b1': _L0_ffn_in['b1'], 'L0_ffn_w2': _L0_ffn_in['w2'], 'L0_ffn_b2': _L0_ffn_in['b2']}
    _x0 = _d['L0_attn_x']
    _d['L0_attn_x'] = jax.random.normal(jax.random.fold_in(jax.random.key(seed), 1), (16, 256, 128), dtype=_x0.dtype)
    del _x0
    return _d

def reference(L0_attn_x, L0_attn_norm_w, L0_attn_norm_b, L0_attn_qkv_w, L0_attn_qkv_b, L0_attn_proj_w, L0_attn_proj_b, L0_ffn_centroids, L0_ffn_ln_g, L0_ffn_ln_b, L0_ffn_w1, L0_ffn_b1, L0_ffn_w2, L0_ffn_b2):

    def _L0_attn_ref(x, norm_w, norm_b, qkv_w, qkv_b, proj_w, proj_b):
        import jax, jax.numpy as jnp
        import numpy as np
        NUM_HEADS = 1
        LN_EPS = 1e-05
        B, L, D = x.shape
        H = NUM_HEADS
        mu = jnp.mean(x, axis=-1, keepdims=True)
        var = jnp.mean(jnp.square(x - mu), axis=-1, keepdims=True)
        h = (x - mu) / jnp.sqrt(var + LN_EPS) * norm_w + norm_b
        qkv = h @ qkv_w.T + qkv_b
        qkv = qkv.reshape(B * H, L // H, 3, D)
        q, k, v = (qkv[..., 0, :], qkv[..., 1, :], qkv[..., 2, :])
        scale = np.float32(1.0 / np.sqrt(L // H))
        w = jax.nn.softmax(jnp.einsum('ncq,nck->nqk', q, k * scale), axis=2)
        a = jnp.einsum('nqk,nck->ncq', w, v)
        a = a.reshape(B, L, D)
        return a @ proj_w.T + proj_b + x

    def _L0_ffn_ref(input_features, centroids, ln_g, ln_b, w1, b1, w2, b2):
        import jax, jax.numpy as jnp
        import numpy as np
        E, D, F = (8, 128, 512)
        B, S = (4, 256)

        def _layernorm(x, g, b, eps=1e-05):
            mu = jnp.mean(x, axis=-1, keepdims=True)
            var = jnp.var(x, axis=-1, keepdims=True)
            return (x - mu) * jax.lax.rsqrt(var + eps) * g + b
        Bf, Sf, Df = input_features.shape
        x = input_features.reshape(-1, Df)
        aff = x @ centroids.T
        assign = jnp.argmax(aff, axis=1)
        order = jnp.argsort(assign)
        xs = x[order]
        es = assign[order]
        alpha = jax.nn.sigmoid(jnp.take_along_axis(aff[order], es[:, None], axis=1))
        nE = centroids.shape[0]
        y = jnp.zeros_like(xs)
        for e in range(nE):
            h = _layernorm(xs, ln_g[e], ln_b[e])
            h = jax.nn.relu(h @ w1[e].T + b1[e])
            ye = xs + h @ w2[e].T + b2[e]
            y = y + jnp.where((es == e)[:, None], ye, 0.0)
        out_sorted = alpha * y + (1.0 - alpha) * xs
        inv = jnp.argsort(order)
        return out_sorted[inv].reshape(Bf, Sf, Df)
    x = L0_attn_x
    x = x + _L0_attn_ref(_layernorm(x, axis=-1), L0_attn_norm_w, L0_attn_norm_b, L0_attn_qkv_w, L0_attn_qkv_b, L0_attn_proj_w, L0_attn_proj_b)
    x = x + _L0_ffn_ref(_layernorm(x, axis=-1), L0_ffn_centroids, L0_ffn_ln_g, L0_ffn_ln_b, L0_ffn_w1, L0_ffn_b1, L0_ffn_w2, L0_ffn_b2)
    return x

_drawn_inputs = setup_inputs


def setup_inputs(seed=0):
    import zlib

    import numpy as np

    out = dict(_drawn_inputs(seed))
    spreads = {'L0_attn_norm_w': (1.0, 0.2),
     'L0_attn_norm_b': (0.0, 0.1),
     'L0_attn_qkv_b': (0.0, 0.1),
     'L0_attn_proj_b': (0.0, 0.1),
     'L0_ffn_ln_g': (1.0, 0.2),
     'L0_ffn_ln_b': (0.0, 0.41),
     'L0_ffn_b1': (0.0, 0.422),
     'L0_ffn_b2': (0.0, 0.305)}
    factors = {}
    for name, (base, spread) in spreads.items():
        noise = np.random.default_rng([zlib.crc32(name.encode()), seed]).standard_normal(out[name].shape)
        drawn = base * np.exp(spread * noise) if base else spread * noise
        out[name] = jnp.asarray(drawn.astype(out[name].dtype))
    for name, factor in factors.items():
        out[name] = (out[name] * factor).astype(out[name].dtype)
    return out
```

```python
from contextlib import ExitStack

import numpy as np

import concourse.bass as bass
from concourse import mybir

P = 128
D = 128
B, L = 16, 256
TOKENS = B * L
E, F = 8, 512
FC = F // P
TILES = TOKENS // P
ST = 4
STEPS = TILES // ST
AW = D + E
OW = AW + E
EPS = 1e-5
SCALE = 1.0 / 16.0
NBLK = TILES + E - 1
CAP = TOKENS + P
ROWS = E * CAP + P
C_HA, C_HB, C_SA, C_SB, C_AL, C_TOK = D, D + 1, D + 2, D + 3, D + 4, D + 5
RW = D + 6
NO_TOKEN = 1 << 20

ALU = mybir.AluOpType
ACT = mybir.ActivationFunctionType
AX = mybir.AxisListType
F32 = mybir.dt.float32
BF16 = mybir.dt.bfloat16
I32 = mybir.dt.int32
U32 = mybir.dt.uint32

A_W, A_P, A_C, A_G, A_B, A_COL = 0, 384, 512, 520, 528, 536
A_END = 539
K_DESC, K_ECAP = 0, ST * E
K_END = 2 * ST * E
T_BLK = 0
T_THR = T_BLK + NBLK * E
T_LOW = T_THR + E * TILES
T_B128 = T_LOW + E * E
T_ECAP = T_B128 + NBLK
T_END = T_ECAP + E


class Step:

    def __init__(self, i, c):
        self.i, self.c = i, c
        self.num = 2 * i + c
        self.par = c % 2
        self.turn = i + c // 2

    def is_first(self):
        return isinstance(self.i, int) and self.num == 0

    def since(self, k):
        return self.c >= k if not isinstance(self.i, int) else self.num >= k

    def plus(self, k):
        return Step(self.i, self.c + k)


class Chain:

    def __init__(self, eng, sem):
        self.eng, self.sem, self.count, self.turns = eng, sem, 0, None

    def link(self, ins):
        self.count += 1
        ins.then_inc(self.sem, 1)
        self.eng.wait_ge(self.sem, self.count if self.turns is None else self.turns * self.per + self.count)

    def loop(self, i, per):
        self.turns, self.per, self.before = i, per, self.count

    def end(self, turns):
        assert self.count - self.before == self.per, self.count - self.before
        self.turns, self.count = None, self.before + turns * self.per


def build(nc, x, attn_w, proj_w, qkv_b, w1, w2, b1, b2, const_f, const_b, ident, token_ids, table_c, filler, out):
    with ExitStack() as ctx:
        def sb(name, shape, dt=F32):
            return ctx.enter_context(nc.sbuf_tensor(name, shape, dt))

        def sem(name):
            return ctx.enter_context(nc.semaphore(name))

        scratch = nc.dram_tensor("rows_by_expert", [ROWS, RW], F32, kind="Internal").ap()

        bank = [ctx.enter_context(nc.psum_tensor(f"bank{k}", [P, 512], F32)) for k in range(6)]
        bank_o = ctx.enter_context(nc.psum_tensor("bank_o", [P, 2, 512], F32))
        ps_t, ps_c, ps_u, ps_s, ps_m, ps_g = bank
        ps_rank = ps_g[:, 288:288 + ST * E]
        ps_xt = [bank[0], bank[1]]
        ps_ha = [bank[2], bank[3]]
        ps_hb = [bank[4], bank[5]]
        ps_y = [bank_o[:, 0, :], bank_o[:, 1, :]]

        x_sb = sb("x_sb", [P, TILES * D])
        aw = sb("aw", [P, A_END])
        pw = sb("pw", [P, D])
        qb = sb("qb", [1, 3 * D])
        w1_sb = sb("w1_sb", [P, E * F])
        w2_sb = sb("w2_sb", [P, E * FC * D])
        b1_sb = sb("b1_sb", [P, E * FC])
        b2_sb = sb("b2_sb", [P, E * D])
        cf = sb("cf", [P, K_END])
        cb = sb("cb", [P, 2 * P], BF16)
        tokid = sb("tokid", [P, TILES], I32)
        tc = sb("tc", [1, T_END])
        fill_sb = sb("fill_sb", [P, RW])
        tri, ones_b = cb[:, 0:P], cb[:, P:2 * P]

        one_d = sb("one_d", [P, P])
        mhalf = sb("mhalf", [P, TILES])
        kcon = sb("kcon", [P, 7, TILES])
        mone = sb("mone", [P, ST])
        nbw = sb("nbw", [P, 1])
        nb_t = sb("nb_t", [P, P])
        pb_t = sb("pb_t", [P, P])
        wt = sb("wt", [P, 3 * D])
        wv = sb("wv", [P, D])
        ic = sb("ic", [P, AW])
        pt = sb("pt", [P, AW])
        pbias = sb("pbias", [P, AW])
        wq_t, wk_t = wt[:, 0:D], wt[:, D:2 * D]
        idt = ic[:, 0:D]

        bn1 = sb("bn1", [P, TILES, 6])
        bn2 = [sb(f"bn2_{k}", [P, ST, 6]) for k in range(2)]
        mom = sb("mom", [P, 6, TILES])
        r1 = sb("r1", [P, TILES])
        rho = sb("rho", [P, TILES])
        hbias = sb("hbias", [P, TILES])
        xs1 = sb("xs1", [P, TILES])
        mr1 = sb("mr1", [P, TILES])
        rfac = sb("rfac", [P, TILES])
        mom2 = sb("mom2", [P, 8, ST])
        rs2 = sb("rs2", [P, 2, ST])
        sc2 = sb("sc2", [P, 3, ST])
        xh = [sb(f"xh_{k}", [P, ST, D]) for k in range(2)]
        xt = [sb(f"xt_{k}", [P, ST * D]) for k in range(2)]
        c_sb = sb("c_sb", [P, 2 * D])
        u_sb = sb("u_sb", [P, 2 * D])
        w_sb = sb("w_sb", [P, 2, D])
        wn_sb = sb("wn_sb", [P, 2, D])
        m_sb = sb("m_sb", [P, 2 * AW])
        g_sb = sb("g_sb", [P, 2, OW])
        smax = sb("smax", [P, 2])
        nmax = sb("nmax", [P, 2])
        den = sb("den", [P, 2])
        rden = sb("rden", [P, 2])
        rows = [sb(f"rows_{k}", [P, ST, RW]) for k in range(2)]
        aff0 = sb("aff0", [P, ST, E])
        aff = sb("aff", [P, ST, E])
        amax = [sb(f"amax_{k}", [P, ST]) for k in range(2)]
        hit = sb("hit", [P, ST, E])
        val = sb("val", [P, ST, E])
        first = sb("first", [P, ST])
        onehot = [sb(f"onehot_{k}", [P, ST, E], BF16) for k in range(2)]
        osum = sb("osum", [P, E])
        acc = [sb(f"acc_{k}", [P, E], BF16) for k in range(2)]
        pos = sb("pos", [P, ST, E])
        posh = sb("posh", [P, ST, E])
        posf = sb("posf", [P, ST])
        slot = [sb(f"slot_{k}", [P, ST], U32) for k in range(2)]
        nlog = [sb(f"nlog_{k}", [P, ST]) for k in range(2)]
        eneg = [sb(f"eneg_{k}", [P, ST]) for k in range(2)]
        epos = sb("epos", [P, ST])

        cnt = sb("cnt", [1, E])
        over = sb("over", [1, E, TILES])
        nblk = sb("nblk", [1, E])
        low = sb("low", [1, E, E])
        cum = sb("cum", [1, E])
        past = sb("past", [1, NBLK, E])
        pastn = sb("pastn", [1, NBLK, E])
        bex = sb("bex", [1, NBLK])
        bcum = sb("bcum", [1, NBLK])
        bst = sb("bst", [1, NBLK])
        bst2 = sb("bst2", [1, NBLK])
        frow_f = sb("frow_f", [1, E])
        fill_row = sb("fill_row", [1, E], I32)
        blk_row = sb("blk_row", [1, NBLK], I32)
        blk_exp = sb("blk_exp", [1, NBLK], I32)

        rin = sb("rin", [P, NBLK * RW])
        hn = [sb(f"hn_{k}", [P, D]) for k in range(2)]
        ht = [sb(f"ht_{k}", [P, P]) for k in range(2)]
        w1_now = [sb(f"w1_now_{k}", [P, F]) for k in range(2)]
        hid = [sb(f"hid_{k}", [P, FC, P]) for k in range(2)]
        base = [sb(f"base_{k}", [P, D]) for k in range(2)]
        base2 = [sb(f"base2_{k}", [P, D]) for k in range(2)]
        ob = [sb(f"ob_{k}", [P, D]) for k in range(2)]
        tix = [sb(f"tix_{k}", [P, 1], U32) for k in range(2)]

        x_in = [sem(f"x_in_{k}") for k in range(2)]
        aw_in, const_in, w1_in, w2_in, small_in = (sem(n) for n in ("aw_in", "const_in", "w1_in", "w2_in", "small_in"))
        set_ready, prep_in, prep_mm, prep_ready = (sem(n) for n in ("set_ready", "prep_in", "prep_mm", "prep_ready"))
        dve_own, pool_own, pool_set = sem("dve_own"), sem("pool_own"), sem("pool_set")
        settled = sem("settled")
        stats1, h_scalars, x1_scalars, xh_ready = sem("stats1"), sem("h_scalars"), sem("x1_scalars"), sem("xh_ready")
        c_done, t_done, u_done, s_done, m_done, g_done, o_done = (sem(n) for n in (
            "c_done", "t_done", "u_done", "s_done", "m_done", "g_done", "o_done"))
        c_ready, xt_ready, u_ready, m_ready, g_ready = (sem(n) for n in (
            "c_ready", "xt_ready", "u_ready", "m_ready", "g_ready"))
        nmax_ready, exp_done, wn_ready = sem("nmax_ready"), sem("exp_done"), sem("wn_ready")
        x1_ready, o_read, stats2, onehot_ready = sem("x1_ready"), sem("o_read"), sem("stats2"), sem("onehot_ready")
        amax_ready = sem("amax_ready")
        acc_ready, rank_done, slot_ready = sem("acc_ready"), sem("rank_done"), sem("slot_ready")
        nlog_ready, eneg_ready = sem("nlog_ready"), sem("eneg_ready")
        row_scalars = sem("row_scalars")
        stored = [sem(f"stored_{k}") for k in range(2)]
        total_done, fill_ready, table_ready, fill_done = (sem(n) for n in (
            "total_done", "fill_ready", "table_ready", "fill_done"))
        row_in = [sem(f"row_in_{k}") for k in range(2)]
        hn_ready, xt2_done, ht_ready, l1_done, relu_a, relu_b = (sem(n) for n in (
            "hn_ready", "xt2_done", "ht_ready", "l1_done", "relu_a", "relu_b"))
        base_ready, base_used, l2_done, ob_ready, tix_ready = (sem(n) for n in (
            "base_ready", "base_used", "l2_done", "ob_ready", "tix_ready"))
        w1_ready = sem("w1_ready")
        out_done = [sem(f"out_done_{k}") for k in range(2)]

        block = ctx.enter_context(nc.Block())

        def x_tile(st, t):
            return x_sb[:, bass.ds(st.num * (ST * D) + t * D, D)]

        PEEL = 4
        LOOP = (STEPS - PEEL) // 2

        def slots(eng, body, chain=None, per=0):
            for c in range(PEEL):
                body(Step(0, c))
            with eng.Fori(0, LOOP) as i:
                if chain:
                    chain.loop(i, per)
                body(Step(i, PEEL))
                body(Step(i, PEEL + 1))
            if chain:
                chain.end(LOOP)
            for c in range(PEEL + 2 * LOOP, STEPS + 2):
                body(Step(0, c))

        def within(st, first, last):
            lo, hi = (st.num, st.num) if isinstance(st.i, int) else (st.c, st.c + 2 * (LOOP - 1))
            assert (first <= lo and hi <= last) or hi < first or lo > last, (first, last, lo, hi)
            return first <= lo and hi <= last

        BLOOP = (NBLK - 5) // 2

        def blocks(eng, body):
            for c in range(3):
                body(Step(0, c))
            with eng.Fori(0, BLOOP) as i:
                body(Step(i, 3))
                body(Step(i, 4))
            for c in range(3 + 2 * BLOOP, NBLK + 1):
                body(Step(0, c))

        def has(st, last):
            return not isinstance(st.i, int) or st.num <= last

        def settle(eng):
            eng.sem_inc(settled, 1)

        def expert(eng, st):
            return eng.value_load(blk_exp[0:1, bass.ds(st.num, 1)], min_val=0, max_val=E - 1)

        @block.sync
        def _(sp):
            sp.dma_start(aw[:], attn_w).then_inc(aw_in, 16)

            def load_x(st):
                src = x[:, bass.ds(st.num * 2, 2)]
                dst = x_sb[:, bass.ds(st.num * (ST * D), ST * D)].rearrange("p (n a) -> p n a", n=2)
                sp.dma_start(dst, src).then_inc(x_in[st.par], 16)

            load_x(Step(0, 0))
            load_x(Step(0, 1))
            with sp.Fori(0, STEPS // 2 - 1) as i:
                for c in range(2, 4):
                    sp.wait_ge(x_in[c % 2], 16 * (i + 1))
                    load_x(Step(i, c))
            sp.wait_ge(const_in, 16 * 6)
            sp.dma_start(scratch[E * CAP:E * CAP + P, :], fill_sb[:]).then_inc(fill_done, 16)
            sp.wait_ge(fill_ready, 1)
            with sp.Fori(0, E) as e:
                r = sp.value_load(fill_row[0:1, bass.ds(e, 1)], min_val=0, max_val=ROWS - P)
                sp.dma_start(scratch[bass.ds(r, P), :], fill_sb[:]).then_inc(fill_done, 16)
            sp.wait_ge(fill_done, 16 * (E + 1))
            for k in range(2):
                sp.wait_ge(stored[k], 16 * ST * (STEPS // 2))
            sp.wait_ge(table_ready, 1)

            def load(st):
                if not has(st, NBLK - 1):
                    return
                if st.since(2):
                    sp.wait_ge(row_in[st.par], 16 * st.turn)
                r = sp.value_load(blk_row[0:1, bass.ds(st.num, 1)], min_val=0, max_val=ROWS - P)
                sp.dma_start(rin[:, bass.ds(st.num * RW, RW)], scratch[bass.ds(r, P), :]).then_inc(row_in[st.par], 16)

            blocks(sp, load)
            sp.wait_ge(out_done[0], 16 * ((NBLK + 1) // 2))
            sp.wait_ge(out_done[1], 16 * (NBLK // 2))

        @block.gpsimd
        def _(pool):
            own = Chain(pool, pool_own)
            pool.memset(mhalf[:], -0.5)
            for n, v in enumerate([0.5, 1.0 / D, 0.25, EPS, 0.0, -1.0, 1.0]):
                pool.memset(kcon[:, n, :], v)
            pool.memset(mone[:], -1.0).then_inc(pool_set, 1)
            pool.wait_ge(pool_set, 1)

            def kc(n, width):
                return kcon[:, n, 0:width]

            def moments(bn, m, width):
                pool.tensor_tensor(m[:, 2, :], bn[:, :, 1], bn[:, :, 4], ALU.add)
                pool.tensor_tensor(m[:, 3, :], bn[:, :, 2], bn[:, :, 5], ALU.add)
                own.link(pool.tensor_tensor(m[:, 4, :], bn[:, :, 1], bn[:, :, 4], ALU.subtract))
                pool.tensor_tensor(m[:, 0, :], m[:, 2, :], kc(0, width), ALU.mult)
                pool.tensor_tensor(m[:, 3, :], m[:, 3, :], kc(1, width), ALU.mult)
                own.link(pool.tensor_tensor(m[:, 5, :], m[:, 4, :], kc(2, width), ALU.mult))
                own.link(pool.tensor_tensor(m[:, 4, :], m[:, 4, :], m[:, 5, :], ALU.mult))
                own.link(pool.tensor_tensor(m[:, 1, :], m[:, 3, :], m[:, 4, :], ALU.add))

            def scalars1():
                pool.wait_ge(stats1, STEPS)
                moments(bn1[:], mom, TILES)
                mean, var = mom[:, 0, :], mom[:, 1, :]
                pool.tensor_scalar(mom[:, 2, :], var, EPS, None, ALU.add)
                own.link(pool.tensor_scalar(mom[:, 3, :], var, 1.0 + EPS, EPS * EPS, ALU.mult, ALU.add))
                own.link(pool.tensor_tensor(rho[:], mom[:, 3, :], mhalf[:], ALU.pow))
                own.link(pool.tensor_tensor(mom[:, 4, :], mean, rho[:], ALU.mult))
                pool.tensor_scalar(hbias[:], mom[:, 4, :], -1.0, 1.0, ALU.mult, ALU.add).then_inc(h_scalars, 1)
                own.link(pool.tensor_tensor(r1[:], mom[:, 2, :], mhalf[:], ALU.pow))
                pool.tensor_tensor(mr1[:], mean, r1[:], ALU.mult)
                pool.tensor_scalar(xs1[:], r1[:], 1.0, None, ALU.add)
                own.link(pool.tensor_tensor(mom[:, 5, :], mom[:, 3, :], rho[:], ALU.mult))
                own.link(pool.tensor_tensor(rfac[:], mom[:, 5, :], xs1[:], ALU.mult))
                pool.drain().then_inc(x1_scalars, 1)

            def scalars2(st):
                pool.wait_ge(stats2, st.num + 1)
                r, k = rows[st.par], st.par
                moments(bn2[k][:], mom2, ST)
                mean, var = mom2[:, 0, :], mom2[:, 1, :]
                own.link(pool.tensor_tensor(mom2[:, 6, :], var, kc(3, ST), ALU.add))
                own.link(pool.tensor_tensor(mom2[:, 5, :], mom2[:, 6, :], kc(3, ST), ALU.mult))
                own.link(pool.tensor_tensor(mom2[:, 7, :], mom2[:, 5, :], var, ALU.add))
                own.link(pool.tensor_tensor(rs2[:], mom2[:, 6:8, :], mhalf[:, 0:2 * ST].rearrange("p (a t) -> p a t", a=2), ALU.pow))
                pool.wait_ge(amax_ready, st.num + 1)
                pool.tensor_tensor(sc2[:, 0, :], rs2[:, 0, :], amax[k][:], ALU.mult)
                pool.tensor_tensor(sc2[:, 1, :], mean, rs2[:, 1, :], ALU.mult)
                own.link(pool.tensor_tensor(sc2[:, 2, :], mean, rs2[:, 0, :], ALU.mult))
                pool.tensor_tensor(nlog[k][:], sc2[:, 0, :], kc(5, ST), ALU.mult).then_inc(nlog_ready, 1)
                own.link(pool.tensor_tensor(sc2[:, 2, :], sc2[:, 2, :], mr1[:, bass.ds(st.num * ST, ST)], ALU.add))
                pool.tensor_tensor(r[:, :, C_SB], sc2[:, 2, :], kc(5, ST), ALU.mult)
                pool.tensor_copy(r[:, :, C_HA], rs2[:, 1, :])
                pool.tensor_scalar(r[:, :, C_HB], sc2[:, 1, :], -1.0, None, ALU.mult)
                pool.tensor_scalar(r[:, :, C_SA], rs2[:, 0, :], 1.0, None, ALU.add).then_inc(row_scalars, 1)

            def store_rows(st):
                k = st.par
                pool.wait_ge(eneg_ready, st.num + 1)
                own.link(pool.tensor_tensor(epos[:], eneg[k][:], kc(6, ST), ALU.add))
                own.link(pool.tensor_tensor(rows[k][:, :, C_AL], epos[:], mone[:], ALU.pow))
                pool.wait_ge(slot_ready, st.num + 1)
                pool.wait_ge(row_scalars, st.num + 1)
                settle(pool)
                for t in range(ST):
                    pool.indirect_dma_start(scratch, bass.IndirectOffsetOnAxis(ap=slot[k][:, t:t + 1], axis=0),
                                            rows[k][:, t, :], None).then_inc(stored[k], 16)

            scalars1()

            def body(st):
                if within(st, 2, STEPS + 1):
                    store_rows(st.plus(-2))
                if within(st, 1, STEPS):
                    scalars2(st.plus(-1))

            slots(pool, body, own, 24)

            def give(st):
                if not st.is_first():
                    b = st.plus(-1)
                    pool.wait_ge(out_done[b.par], 16 * b.turn)
                    settle(pool)
                    pool.tensor_copy(tix[b.par][:], rin[:, bass.ds(b.num * RW + C_TOK, 1)].bitcast(U32)).then_inc(tix_ready, 1)
                    pool.wait_ge(tix_ready, b.num + 1)
                    pool.wait_ge(ob_ready, b.num + 1)
                    settle(pool)
                    pool.indirect_dma_start(out, bass.IndirectOffsetOnAxis(ap=tix[b.par][:], axis=0), ob[b.par][:], None,
                                            bounds_check=TOKENS - 1, oob_is_err=False).then_inc(out_done[b.par], 16)

            pool.wait_ge(row_in[0], 16)
            blocks(pool, give)

        @block.scalar
        def _(act):
            act.dma_start(cf[:], const_f).then_inc(const_in, 16)
            act.dma_start(ic[:, 0:D], ident).then_inc(const_in, 16)
            act.dma_start(cb[:], const_b).then_inc(const_in, 16)
            act.dma_start(tokid[:], token_ids).then_inc(const_in, 16)
            act.dma_start(tc[:], table_c).then_inc(const_in, 16)
            act.dma_start(fill_sb[:], filler).then_inc(const_in, 16)
            act.dma_start(pw[:], proj_w).then_inc(small_in, 16)
            act.dma_start(qb[:], qkv_b).then_inc(small_in, 16)
            act.dma_start(b1_sb[:], b1).then_inc(w1_in, 16)
            act.dma_start(w1_sb[:], w1).then_inc(w1_in, 16)
            act.dma_start(b2_sb[:], b2.partition_broadcast(P)).then_inc(w2_in, 16)
            act.dma_start(w2_sb[:], w2).then_inc(w2_in, 16)

            def normalise(st):
                if st.is_first():
                    act.wait_ge(h_scalars, 1)
                if st.since(1):
                    act.wait_ge(t_done, st.num - 1)
                for t in range(ST):
                    col = st.num * ST + t
                    last = act.activation(xh[st.par][:, t, :], x_tile(st, t), ACT.Identity,
                                          bias=hbias[:, bass.ds(col, 1)], scale=rho[:, bass.ds(col, 1)])
                last.then_inc(xh_ready, 1)

            def body(st):
                if within(st, 2, STEPS + 1):
                    q = st.plus(-2)
                    act.wait_ge(nlog_ready, q.num + 1)
                    act.activation(eneg[q.par][:], nlog[q.par][:], ACT.Exp).then_inc(eneg_ready, 1)
                if within(st, 0, STEPS - 1):
                    normalise(st)
                    act.wait_ge(c_done, st.num + 1)
                    act.wait_ge(u_done, st.num)
                    act.copy(c_sb[:], ps_c[:, 0:2 * D]).then_inc(c_ready, 1)
                if within(st, 1, STEPS):
                    act.wait_ge(m_done, st.num)
                    act.wait_ge(g_done, st.num - 1)
                    act.copy(m_sb[:], ps_m[:, 0:2 * AW]).then_inc(m_ready, 1)
                if within(st, 0, STEPS - 1):
                    act.wait_ge(t_done, st.num + 1)
                    if st.since(1):
                        act.wait_ge(o_done, st.num - 1)
                    act.copy(xt[st.par][:], ps_t[:]).then_inc(xt_ready, 1)
                    act.wait_ge(nmax_ready, st.num + 1)
                    act.wait_ge(wn_ready, st.num)
                    for b in range(2):
                        last = act.activation(w_sb[:, b, :], ps_s[:, b * D:(b + 1) * D], ACT.Exp, bias=nmax[:, b:b + 1],
                                              scale=SCALE, accum_out=den[:, b:b + 1])
                    last.then_inc(exp_done, 1)

            slots(act, body)

            def turn(st):
                act.wait_ge(xt2_done, st.num + 1)
                if st.since(1):
                    act.wait_ge(l1_done, st.num - 1)
                settle(act)
                e = expert(act, st)
                act.activation(ht[st.par][:], ps_xt[st.par][:, 0:P], ACT.Identity, bias=aw[:, bass.ds(e + A_B, 1)],
                               scale=aw[:, bass.ds(e + A_G, 1)]).then_inc(ht_ready, 1)

            def block_body(st):
                if st.is_first():
                    turn(st)
                if has(st.plus(1), NBLK - 1):
                    turn(st.plus(1))
                if has(st, NBLK - 1):
                    row = st.num * RW
                    if st.since(1):
                        act.wait_ge(base_used, st.num - 1)
                    act.activation(base[st.par][:], rin[:, bass.ds(row, D)], ACT.Identity, bias=rin[:, bass.ds(row + C_SB, 1)],
                                   scale=rin[:, bass.ds(row + C_SA, 1)]).then_inc(base_ready, 1)
                    act.wait_ge(l1_done, st.num + 1)
                    if st.since(1):
                        act.wait_ge(l2_done, st.num - 1)
                    settle(act)
                    e = expert(act, st)
                    for c in range(2):
                        last = act.activation(hid[st.par][:, c, :], ps_ha[st.par][:, c * P:(c + 1) * P], ACT.Relu,
                                              bias=b1_sb[:, bass.ds(e * FC + c, 1)])
                    last.then_inc(relu_a, 1)

            act.wait_ge(table_ready, 1)
            act.wait_ge(row_in[0], 16)
            act.wait_ge(w1_in, 32)
            blocks(act, block_body)

        @block.vector
        def _(dve):
            own = Chain(dve, dve_own)
            dve.memset(one_d[:], 1.0 / D)
            dve.memset(acc[0][:], 0.0)
            dve.wait_ge(aw_in, 16)
            own.link(dve.tensor_tensor(nbw[:], aw[:, A_COL + 1:A_COL + 2], aw[:, A_COL:A_COL + 1], ALU.subtract))
            dve.tensor_scalar(nb_t[:], one_d[:], nbw[:], None, ALU.mult)
            dve.tensor_scalar(pb_t[:], one_d[:], aw[:, A_COL + 2:A_COL + 3], None, ALU.mult).then_inc(prep_in, 1)
            dve.wait_ge(prep_mm, 1)
            dve.scalar_tensor_tensor(out=wt[:], in0=aw[:, 0:3 * D], scalar=aw[:, A_COL:A_COL + 1], in1=bank[0][:, 0:3 * D],
                                     op0=ALU.mult, op1=ALU.add).then_inc(prep_in, 1)
            dve.wait_ge(prep_mm, 2)
            dve.tensor_tensor(ic[:, D:AW], aw[:, A_C:A_C + E], bank[1][:, 0:E], ALU.subtract).then_inc(prep_in, 1)
            dve.tensor_copy(pt[:, 0:D], aw[:, A_P:A_P + D])
            dve.wait_ge(prep_in, 3)
            for b in range(2):
                dve.tensor_copy(g_sb[:, b, AW:OW], ic[:, D:AW])
            dve.wait_ge(prep_mm, 3)
            dve.tensor_copy(wv[:], bank[2][:, 0:D])
            dve.wait_ge(prep_mm, 4)
            dve.tensor_copy(pbias[:], bank[3][:, 0:AW])
            dve.tensor_copy(pt[:, D:AW], bank[4][:, 0:E]).then_inc(prep_ready, 1)
            dve.wait_ge(prep_ready, 1)
            dve.wait_ge(const_in, 16 * 6)

            with dve.Fori(0, STEPS // 2) as i:
                for k in range(2):
                    st = Step(i, k)
                    dve.wait_ge(x_in[k], 16 * (i + 1))
                    for t in range(ST):
                        last = dve.bn_stats(bn1[:, bass.ds(st.num * ST + t, 1), :].rearrange("p a s -> p (a s)"), x_tile(st, t))
                    last.then_inc(stats1, 1)

            def softmax_max(st):
                dve.wait_ge(s_done, st.num + 1)
                own.link(dve.tensor_reduce(smax[:], ps_s[:, 0:2 * D].rearrange("p (b k) -> p b k", b=2), AX.X, ALU.max))
                dve.wait_ge(exp_done, st.num)
                dve.tensor_scalar(nmax[:], smax[:], -SCALE, None, ALU.mult).then_inc(nmax_ready, 1)

            def softmax_weights(st):
                dve.wait_ge(exp_done, st.num + 1)
                own.link(dve.reciprocal(rden[:], den[:]))
                dve.wait_ge(m_done, st.num)
                for b in range(2):
                    last = dve.tensor_scalar(wn_sb[:, b, :], w_sb[:, b, :], rden[:, b:b + 1], None, ALU.mult)
                last.then_inc(wn_ready, 1)

            def residual(st):
                k = st.par
                r = rows[k]
                dve.wait_ge(o_done, st.num + 1)
                if st.since(2):
                    dve.wait_ge(stored[k], 16 * ST * st.turn)
                for t in range(ST):
                    col = st.num * ST + t
                    last = dve.scalar_tensor_tensor(out=r[:, t, 0:D], in0=x_tile(st, t), scalar=xs1[:, bass.ds(col, 1)],
                                                    in1=bank_o[:, t // 2, (t % 2) * OW:(t % 2) * OW + D],
                                                    op0=ALU.mult, op1=ALU.add)
                last.then_inc(x1_ready, 1)
                both = bank_o[:, :, 0:2 * OW].rearrange("p b (j c) -> p b j c", j=2)
                tiles = "p (b j) c -> p b j c"
                fac = rfac[:, bass.ds(st.num * ST, ST)].rearrange("p (b j) -> p b j", b=2).unsqueeze(3).to_broadcast([P, 2, 2, E])
                own.link(dve.tensor_tensor(aff0[:].rearrange(tiles, b=2), both[:, :, :, AW:OW], fac, ALU.mult))
                dve.tensor_tensor(aff[:].rearrange(tiles, b=2), both[:, :, :, D:AW], aff0[:].rearrange(tiles, b=2),
                                  ALU.add).then_inc(o_read, 1)
                dve.tensor_copy(r[:, :, C_TOK].bitcast(I32), tokid[:, bass.ds(st.num * ST, ST)])
                dve.wait_ge(x1_ready, st.num + 1)
                for t in range(ST):
                    last = dve.bn_stats(bn2[k][:, t, :], r[:, t, 0:D])
                last.then_inc(stats2, 1)
                dve.wait_ge(o_read, st.num + 1)
                dve.tensor_reduce(amax[k][:], aff[:], AX.X, ALU.max).then_inc(amax_ready, 1)
                dve.wait_ge(amax_ready, st.num + 1)
                own.link(dve.tensor_tensor(hit[:], aff[:], amax[k][:].unsqueeze(2).to_broadcast([P, ST, E]), ALU.is_equal))
                desc = cf[:, K_DESC:K_DESC + ST * E].rearrange("p (t e) -> p t e", t=ST)
                own.link(dve.tensor_tensor(val[:], hit[:], desc, ALU.mult))
                own.link(dve.tensor_reduce(first[:], val[:], AX.X, ALU.max))
                dve.tensor_tensor(onehot[k][:], desc, first[:].unsqueeze(2).to_broadcast([P, ST, E]),
                                  ALU.is_equal).then_inc(onehot_ready, 1)
                dve.wait_ge(onehot_ready, st.num + 1)
                own.link(dve.tensor_reduce(osum[:], onehot[k][:].rearrange("p t e -> p e t"), AX.X, ALU.add))
                dve.wait_ge(rank_done, st.num)
                dve.tensor_tensor(acc[1 - k][:], acc[k][:], osum[:], ALU.add).then_inc(acc_ready, 1)

            def places(st):
                k = st.par
                dve.wait_ge(rank_done, st.num + 1)
                flat = "p t e -> p (t e)"
                own.link(dve.tensor_tensor(pos[:].rearrange(flat), ps_rank, cf[:, K_ECAP:K_ECAP + ST * E], ALU.add))
                own.link(dve.tensor_tensor(posh[:], pos[:], onehot[k][:], ALU.mult))
                own.link(dve.tensor_reduce(posf[:], posh[:], AX.X, ALU.add))
                dve.tensor_copy(slot[k][:], posf[:]).then_inc(slot_ready, 1)

            def body(st):
                if within(st, 0, STEPS - 1):
                    dve.wait_ge(u_done, st.num + 1)
                    dve.wait_ge(s_done, st.num)
                    dve.tensor_copy(u_sb[:], ps_u[:, 0:2 * D]).then_inc(u_ready, 1)
                if within(st, 1, STEPS):
                    dve.wait_ge(g_done, st.num)
                    dve.wait_ge(o_done, st.num - 1)
                    dve.tensor_tensor(g_sb[:, :, 0:AW], ps_g[:, 0:2 * AW].rearrange("p (b c) -> p b c", b=2),
                                      pbias[:].unsqueeze(1).to_broadcast([P, 2, AW]), ALU.add).then_inc(g_ready, 1)
                if within(st, 0, STEPS - 1):
                    softmax_max(st)
                if within(st, 2, STEPS + 1):
                    places(st.plus(-2))
                if within(st, 0, STEPS - 1):
                    softmax_weights(st)
                if within(st, 1, STEPS):
                    if st.c == 1 and isinstance(st.i, int):
                        dve.wait_ge(x1_scalars, 1)
                    residual(st.plus(-1))

            slots(dve, body, own, 20)

            dve.wait_ge(total_done, 1)
            own.link(dve.tensor_copy(cnt[:], bank[0][0:1, 0:E]))
            own.link(dve.tensor_tensor(frow_f[:], cnt[:], tc[:, T_ECAP:T_ECAP + E], ALU.add))
            dve.tensor_copy(fill_row[:], frow_f[:]).then_inc(fill_ready, 1)
            thr = tc[:, T_THR:T_THR + E * TILES].rearrange("p (e j) -> p e j", e=E)
            own.link(dve.tensor_tensor(over[:], cnt[:].unsqueeze(2).to_broadcast([1, E, TILES]), thr, ALU.is_gt))
            own.link(dve.tensor_reduce(nblk[:], over[:], AX.X, ALU.add))
            lower = tc[:, T_LOW:T_LOW + E * E].rearrange("p (e j) -> p e j", e=E)
            own.link(dve.tensor_tensor(low[:], nblk[:].unsqueeze(1).to_broadcast([1, E, E]), lower, ALU.mult))
            own.link(dve.tensor_reduce(cum[:], low[:], AX.X, ALU.add))
            blk = tc[:, T_BLK:T_BLK + NBLK * E].rearrange("p (b e) -> p b e", b=NBLK)
            own.link(dve.tensor_tensor(past[:], blk, cum[:].unsqueeze(1).to_broadcast([1, NBLK, E]), ALU.is_ge))
            own.link(dve.tensor_tensor(pastn[:], past[:], nblk[:].unsqueeze(1).to_broadcast([1, NBLK, E]), ALU.mult))
            own.link(dve.tensor_reduce(bex[:], past[:], AX.X, ALU.add))
            own.link(dve.tensor_reduce(bcum[:], pastn[:], AX.X, ALU.add))
            own.link(dve.scalar_tensor_tensor(out=bst[:], in0=bcum[:], scalar=-float(P), in1=tc[:, T_B128:T_B128 + NBLK],
                                              op0=ALU.mult, op1=ALU.add))
            own.link(dve.scalar_tensor_tensor(out=bst2[:], in0=bex[:], scalar=float(CAP), in1=bst[:], op0=ALU.mult, op1=ALU.add))
            own.link(dve.tensor_scalar(blk_row[:], bst2[:], float(E * CAP), None, ALU.min))
            dve.tensor_scalar(blk_exp[:], bex[:], float(E - 1), None, ALU.min).then_inc(table_ready, 1)

            def whiten(st):
                dve.wait_ge(row_in[st.par], 16 * (st.turn + 1))
                if st.since(1):
                    dve.wait_ge(xt2_done, st.num - 1)
                row = st.num * RW
                dve.tensor_scalar(hn[st.par][:], rin[:, bass.ds(row, D)], rin[:, bass.ds(row + C_HA, 1)],
                                  rin[:, bass.ds(row + C_HB, 1)], ALU.mult, ALU.add).then_inc(hn_ready, 1)

            def fetch_w1(st):
                e = expert(dve, st)
                if st.since(1):
                    dve.wait_ge(l1_done, st.num - 1)
                dve.tensor_copy(w1_now[st.par][:], w1_sb[:, bass.ds(e * F, F)]).then_inc(w1_ready, 1)

            def block_body(st):
                if st.is_first():
                    whiten(st)
                    whiten(st.plus(1))
                    fetch_w1(st)
                if has(st.plus(1), NBLK - 1):
                    fetch_w1(st.plus(1))
                if has(st.plus(2), NBLK - 1):
                    whiten(st.plus(2))
                if has(st, NBLK - 1):
                    e = expert(dve, st)
                    dve.wait_ge(l1_done, st.num + 1)
                    if st.since(1):
                        dve.wait_ge(l2_done, st.num - 1)
                    for c in range(2, FC):
                        last = dve.tensor_scalar(hid[st.par][:, c, :], ps_hb[st.par][:, (c - 2) * P:(c - 1) * P],
                                                 b1_sb[:, bass.ds(e * FC + c, 1)], 0.0, ALU.add, ALU.max)
                    last.then_inc(relu_b, 1)
                    dve.wait_ge(base_ready, st.num + 1)
                    if st.since(1):
                        dve.wait_ge(ob_ready, st.num - 1)
                    dve.scalar_tensor_tensor(out=base2[st.par][:], in0=b2_sb[:, bass.ds(e * D, D)],
                                             scalar=rin[:, bass.ds(st.num * RW + C_AL, 1)], in1=base[st.par][:],
                                             op0=ALU.mult, op1=ALU.add).then_inc(base_used, 1)
                if not st.is_first():
                    b = st.plus(-1)
                    dve.wait_ge(l2_done, b.num + 1)
                    dve.wait_ge(base_used, b.num + 1)
                    dve.wait_ge(out_done[b.par], 16 * b.turn)
                    dve.scalar_tensor_tensor(out=ob[b.par][:], in0=ps_y[b.par][:, 0:D],
                                             scalar=rin[:, bass.ds(b.num * RW + C_AL, 1)], in1=base2[b.par][:],
                                             op0=ALU.mult, op1=ALU.add).then_inc(ob_ready, 1)

            dve.wait_ge(w1_in, 32)
            dve.wait_ge(w2_in, 32)
            dve.wait_ge(table_ready, 1)
            blocks(dve, block_body)

        @block.tensor
        def _(pe):
            def mm(out, lhs, rhs, start=True, stop=True):
                return pe.matmul(out, lhs, rhs, start=start, stop=stop)

            pe.wait_ge(prep_in, 1)
            pe.wait_ge(small_in, 32)
            mm(bank[0][:, 0:3 * D], nb_t[:], aw[:, 0:3 * D], stop=False)
            mm(bank[0][:, 0:3 * D], one_d[0:1, :], qb[:], start=False).then_inc(prep_mm, 1)
            mm(bank[1][:, 0:E], one_d[:], aw[:, A_C:A_C + E]).then_inc(prep_mm, 1)
            pe.wait_ge(const_in, 16 * 6)
            pe.wait_ge(prep_in, 3)
            pe.transpose(bank[2][:, 0:D], wt[:, 2 * D:3 * D], idt).then_inc(prep_mm, 1)
            mm(bank[3][:, 0:AW], pb_t[:], ic[:])
            mm(bank[4][:, 0:E], pw[:], ic[:, D:AW]).then_inc(prep_mm, 1)
            pe.wait_ge(prep_ready, 1)

            def body(st):
                k = st.par
                if within(st, 0, STEPS - 1):
                    pe.wait_ge(xh_ready, st.num + 1)
                    pe.wait_ge(c_ready, st.num)
                    for b in range(2):
                        for j in range(2):
                            h = xh[k][:, 2 * b + j, :]
                            last = mm(ps_c[:, b * D:(b + 1) * D], h, h, start=(j == 0), stop=(j == 1))
                    last.then_inc(c_done, 1)
                if within(st, 1, STEPS):
                    pe.wait_ge(wn_ready, st.num)
                    pe.wait_ge(m_ready, st.num - 1)
                    for b in range(2):
                        last = mm(ps_m[:, b * AW:(b + 1) * AW], wn_sb[:, b, :], pt[:])
                    last.then_inc(m_done, 1)
                if within(st, 0, STEPS - 1):
                    pe.wait_ge(xt_ready, st.num)
                    for t in range(ST):
                        last = pe.transpose(ps_t[:, t * P:(t + 1) * P], xh[k][:, t, :], idt)
                    last.then_inc(t_done, 1)
                    pe.wait_ge(c_ready, st.num + 1)
                    pe.wait_ge(u_ready, st.num)
                    for b in range(2):
                        last = mm(ps_u[:, b * D:(b + 1) * D], c_sb[:, b * D:(b + 1) * D], wk_t)
                    last.then_inc(u_done, 1)
                if within(st, 1, STEPS):
                    pe.wait_ge(m_ready, st.num)
                    pe.wait_ge(g_ready, st.num - 1)
                    mm(ps_g[:, 0:2 * AW], wv[:], m_sb[:]).then_inc(g_done, 1)
                if within(st, 2, STEPS + 1):
                    q = st.plus(-2)
                    oh = onehot[q.par][:].rearrange("p t e -> p (t e)")
                    pe.wait_ge(onehot_ready, q.num + 1)
                    pe.wait_ge(acc_ready, q.num + 1)
                    if within(st, 1, STEPS):
                        pe.wait_ge(g_ready, st.num)
                    mm(ps_rank, tri, oh, stop=False)
                    for t in range(1, ST):
                        mm(ps_rank[:, t * E:ST * E], ones_b, oh[:, 0:(ST - t) * E], start=False, stop=False)
                    mm(ps_rank, ones_b, acc[q.par][:].unsqueeze(1).to_broadcast([P, ST, E]), start=False).then_inc(rank_done, 1)
                if within(st, 0, STEPS - 1):
                    pe.wait_ge(u_ready, st.num + 1)
                    pe.wait_ge(exp_done, st.num)
                    mm(ps_s[:, 0:2 * D], wq_t, u_sb[:]).then_inc(s_done, 1)
                if within(st, 1, STEPS):
                    q = st.plus(-1)
                    pe.wait_ge(g_ready, st.num)
                    pe.wait_ge(xt_ready, st.num)
                    pe.wait_ge(o_read, st.num - 1)
                    pe.wait_ge(x1_ready, st.num - 1)
                    for t in range(ST):
                        last = mm(bank_o[:, t // 2, (t % 2) * OW:(t % 2 + 1) * OW], xt[q.par][:, t * P:(t + 1) * P],
                                  g_sb[:, t // 2, :])
                    last.then_inc(o_done, 1)

            slots(pe, body)
            pe.wait_ge(acc_ready, STEPS)
            mm(bank[0][:, 0:E], ones_b, acc[0][:]).then_inc(total_done, 1)

            def turn(st):
                pe.wait_ge(hn_ready, st.num + 1)
                if st.since(1):
                    pe.wait_ge(ht_ready, st.num - 1)
                pe.transpose(ps_xt[st.par][:, 0:P], hn[st.par][:], idt).then_inc(xt2_done, 1)

            def block_body(st):
                if st.is_first():
                    turn(st)
                if has(st.plus(1), NBLK - 1):
                    turn(st.plus(1))
                if has(st, NBLK - 1):
                    pe.wait_ge(ht_ready, st.num + 1)
                    pe.wait_ge(w1_ready, st.num + 1)
                    if st.since(1):
                        pe.wait_ge(relu_a, st.num - 1)
                        pe.wait_ge(relu_b, st.num - 1)
                    for c in range(FC):
                        half = ps_ha if c < 2 else ps_hb
                        last = mm(half[st.par][:, (c % 2) * P:(c % 2 + 1) * P], w1_now[st.par][:, c * P:(c + 1) * P], ht[st.par][:])
                    last.then_inc(l1_done, 1)
                if not st.is_first():
                    b = st.plus(-1)
                    e = expert(pe, b)
                    pe.wait_ge(relu_a, b.num + 1)
                    pe.wait_ge(relu_b, b.num + 1)
                    if b.since(1):
                        pe.wait_ge(ob_ready, b.num - 1)
                    for c in range(FC):
                        last = mm(ps_y[b.par][:, 0:D], hid[b.par][:, c, :], w2_sb[:, bass.ds((e * FC + c) * D, D)],
                                  start=(c == 0), stop=(c == FC - 1))
                    last.then_inc(l2_done, 1)

            pe.wait_ge(table_ready, 1)
            pe.wait_ge(w2_in, 32)
            blocks(pe, block_body)


def kernel(L0_attn_x, L0_attn_norm_w, L0_attn_norm_b, L0_attn_qkv_w, L0_attn_qkv_b, L0_attn_proj_w, L0_attn_proj_b,
           L0_ffn_centroids, L0_ffn_ln_g, L0_ffn_ln_b, L0_ffn_w1, L0_ffn_b1, L0_ffn_w2, L0_ffn_b2):
    import concourse.bacc as bacc
    from concourse.bass_utils import run_bass_kernel_spmd

    f = np.float32
    attn_w = np.concatenate(
        [L0_attn_qkv_w.T, L0_attn_proj_w.T, L0_ffn_centroids.T, L0_ffn_ln_g.T, L0_ffn_ln_b.T,
         L0_attn_norm_w[:, None], L0_attn_norm_b[:, None], L0_attn_proj_b[:, None]], axis=1)
    arrays = {
        "x": np.reshape(L0_attn_x, (B, P, 2, D)).transpose(1, 0, 2, 3).reshape(P, B, 2 * D),
        "attn_w": attn_w,
        "proj_w": L0_attn_proj_w,
        "qkv_b": L0_attn_qkv_b[None, :],
        "w1": L0_ffn_w1.transpose(2, 0, 1).reshape(D, E * F),
        "w2": L0_ffn_w2.reshape(E, D, FC, P).transpose(3, 0, 2, 1).reshape(P, E * FC * D),
        "b1": L0_ffn_b1.reshape(E * FC, P).T,
        "b2": L0_ffn_b2.reshape(E * D),
    }
    import ml_dtypes
    eight = np.arange(E)
    const_f = np.zeros((P, K_END), f)
    const_f[:, K_DESC:K_DESC + ST * E] = np.tile(E - eight, ST)
    const_f[:, K_ECAP:K_ECAP + ST * E] = np.tile(eight * CAP, ST)
    p, m = np.arange(P)[:, None], np.arange(P)[None, :]
    const_b = np.concatenate([p < m, np.ones((P, P))], axis=1).astype(ml_dtypes.bfloat16)
    tile = np.arange(TILES)[None, :]
    filler = np.zeros((P, RW), np.int32)
    filler[:, C_TOK] = NO_TOKEN
    table = np.zeros((1, T_END), f)
    table[0, T_BLK:T_BLK + NBLK * E] = np.repeat(np.arange(NBLK), E)
    table[0, T_THR:T_THR + E * TILES] = np.tile(np.arange(TILES) * P, E)
    table[0, T_LOW:T_LOW + E * E] = (eight[None, :] <= eight[:, None]).reshape(-1)
    table[0, T_B128:T_B128 + NBLK] = np.arange(NBLK) * P
    table[0, T_ECAP:T_ECAP + E] = eight * CAP
    arrays.update({
        "const_f": const_f, "const_b": const_b, "ident": np.eye(P, dtype=f),
        "token_ids": (tile // 2 * L + 2 * p + tile % 2).astype(np.int32),
        "table_c": table, "filler": filler.view(f),
    })
    nc = bacc.Bacc("TRN2", target_bir_lowering=False, num_devices=1)
    feed, args = {}, []
    for name, a in arrays.items():
        a = np.ascontiguousarray(a)
        feed[f"in_{name}"] = a
        args.append(nc.dram_tensor(f"in_{name}", a.shape, mybir.dt.from_np(a.dtype), kind="ExternalInput").ap())
    args.append(nc.dram_tensor("out", (TOKENS, D), F32, kind="ExternalOutput").ap())
    build(nc, *args)
    r = run_bass_kernel_spmd(nc, [feed], core_ids=[0])
    return np.reshape(r.results[0]["out"], (B, L, D))
```

```python
from contextlib import ExitStack

import numpy as np

import concourse.bass as bass
from concourse import mybir

P = 128
D = 128
B, L = 16, 256
TOKENS = B * L
E, F = 8, 512
FC = F // P
TILES = TOKENS // P
ST = 4
STEPS = TILES // ST
AW = D + E
OW = AW + E
EPS = 1e-5
SCALE = 1.0 / 16.0
NBLK = TILES + E - 1
CAP = TOKENS + P
ROWS = E * CAP + P
C_HA, C_HB, C_SA, C_SB, C_AL, C_TOK = D, D + 1, D + 2, D + 3, D + 4, D + 5
RW = D + 6
NO_TOKEN = 1 << 20
ACT_FC = 2
NROW = 4

ALU = mybir.AluOpType
ACT = mybir.ActivationFunctionType
AX = mybir.AxisListType
F32 = mybir.dt.float32
BF16 = mybir.dt.bfloat16
I32 = mybir.dt.int32
U32 = mybir.dt.uint32

A_W, A_P, A_C, A_G, A_B, A_COL = 0, 384, 512, 520, 528, 536
A_END = 539
T_BLK = 0
T_THR = T_BLK + NBLK * E
T_LOW = T_THR + E * TILES
T_B128 = T_LOW + E * E
T_ECAP = T_B128 + NBLK
T_END = T_ECAP + E


GROUPS = [(0, 1), (2, 3), (4, 5), (6,), (7,)]
GROUP_OF = {g[-1]: n for n, g in enumerate(GROUPS)}
WMAX = ST * max(len(g) for g in GROUPS)
K_DESC, K_ECAP = 0, WMAX * E
K_END = 2 * WMAX * E
MAGIC = float(0x5F3759DF)


class Chain:

    def __init__(self, eng, sem):
        self.eng, self.sem, self.count = eng, sem, 0

    def mark(self, ins):
        self.count += 1
        ins.then_inc(self.sem, 1)

    def ready(self):
        self.eng.wait_ge(self.sem, self.count)

    def link(self, ins):
        self.mark(ins)
        self.ready()


def build(nc, x, attn_w, proj_w, qkv_b, w1, w2, b1, b2, const_f, const_b, ident, token_ids, table_c, filler, out):
    with ExitStack() as ctx:
        def sb(name, shape, dt=F32):
            return ctx.enter_context(nc.sbuf_tensor(name, shape, dt))

        def sem(name):
            return ctx.enter_context(nc.semaphore(name))

        scratch = nc.dram_tensor("rows_by_expert", [ROWS, RW], F32, kind="Internal").ap()

        bank = [ctx.enter_context(nc.psum_tensor(f"bank{k}", [P, 512], F32)) for k in range(6)]
        bank_o = ctx.enter_context(nc.psum_tensor("bank_o", [P, 2, 512], F32))
        ps_t, ps_c, ps_u, ps_s, ps_m, ps_g = bank
        ps_rank = ps_g[:, 288:288 + WMAX * E]
        ps_xt = [bank[0], bank[1]]
        ps_ha = [bank[2], bank[3]]
        ps_hb = [bank[4], bank[5]]
        ps_y = [bank_o[:, 0, :], bank_o[:, 1, :]]

        x_sb = sb("x_sb", [P, TILES * D])
        aw = sb("aw", [P, A_END])
        pw = sb("pw", [P, D])
        qb = sb("qb", [1, 3 * D])
        w1_sb = sb("w1_sb", [P, E * F])
        w2_sb = sb("w2_sb", [P, E * FC * D])
        b1_sb = sb("b1_sb", [P, E * FC])
        b2_sb = sb("b2_sb", [P, E * D])
        cf = sb("cf", [P, K_END])
        cb = sb("cb", [P, 2 * P], BF16)
        tokid = sb("tokid", [P, TILES], I32)
        tc = sb("tc", [1, T_END])
        fill_sb = sb("fill_sb", [P, RW])
        tri, ones_b = cb[:, 0:P], cb[:, P:2 * P]

        one_d = sb("one_d", [P, P])
        nbw = sb("nbw", [P, 1])
        nb_t = sb("nb_t", [P, P])
        pb_t = sb("pb_t", [P, P])
        wt = sb("wt", [P, 3 * D])
        wv = sb("wv", [P, D])
        ic = sb("ic", [P, AW])
        pt = sb("pt", [P, AW])
        pbias = sb("pbias", [P, AW])
        wq_t, wk_t = wt[:, 0:D], wt[:, D:2 * D]
        idt = ic[:, 0:D]

        bn1 = sb("bn1", [P, TILES, 6])
        mom1 = sb("mom1", [P, 4, TILES])
        var1 = sb("var1", [P, 2, TILES])
        rs1 = sb("rs1", [P, 2, TILES])
        nw1 = sb("nw1", [P, 2, TILES])
        hbias = sb("hbias", [P, TILES])
        xs1 = sb("xs1", [P, TILES])
        mr1 = sb("mr1", [P, TILES])
        rfac = sb("rfac", [P, TILES])

        xh = [sb(f"xh_{k}", [P, ST, D]) for k in range(2)]
        xt = [sb(f"xt_{k}", [P, ST * D]) for k in range(2)]
        c_sb = sb("c_sb", [P, 2 * D])
        u_sb = sb("u_sb", [P, 2 * D])
        w_sb = sb("w_sb", [P, 2, D])
        wn_sb = sb("wn_sb", [P, 2, D])
        m_sb = sb("m_sb", [P, 2 * AW])
        g_sb = sb("g_sb", [P, 2, OW])
        smax = sb("smax", [P, 2])
        nmax = sb("nmax", [P, 2])
        den = sb("den", [P, 2])
        rden = sb("rden", [P, 2])

        rows = sb("rows", [P, TILES, RW])
        bn2 = sb("bn2", [P, TILES, 6])
        mom2 = sb("mom2", [P, 4, TILES])
        var2 = sb("var2", [P, 2, TILES])
        rs2 = sb("rs2", [P, 2, TILES])
        nw2 = sb("nw2", [P, 2, TILES])
        msb = sb("msb", [P, TILES])
        nlog = sb("nlog", [P, TILES])
        eneg = sb("eneg", [P, TILES])
        epos = sb("epos", [P, TILES])
        aff0 = sb("aff0", [P, TILES, E])
        aff = sb("aff", [P, TILES, E])
        amax = sb("amax", [P, TILES])
        hit = sb("hit", [P, TILES, E])
        val = sb("val", [P, TILES, E])
        first = sb("first", [P, TILES])
        onehot = sb("onehot", [P, TILES, E], BF16)
        osum = sb("osum", [P, len(GROUPS), E])
        acc = sb("acc", [P, len(GROUPS) + 1, E], BF16)
        pos = sb("pos", [P, TILES, E])
        posh = sb("posh", [P, TILES, E])
        posf = sb("posf", [P, TILES])
        slot = sb("slot", [P, TILES], U32)

        cnt = sb("cnt", [1, E])
        over = sb("over", [1, E, TILES])
        nblk = sb("nblk", [1, E])
        low = sb("low", [1, E, E])
        cum = sb("cum", [1, E])
        past = sb("past", [1, NBLK, E])
        pastn = sb("pastn", [1, NBLK, E])
        bex = sb("bex", [1, NBLK])
        bcum = sb("bcum", [1, NBLK])
        bst = sb("bst", [1, NBLK])
        bst2 = sb("bst2", [1, NBLK])
        frow_f = sb("frow_f", [1, E])
        fill_row = sb("fill_row", [1, E], I32)
        blk_row = sb("blk_row", [1, NBLK], I32)
        blk_exp = sb("blk_exp", [1, NBLK], I32)

        rin = sb("rin", [P, NBLK, RW])
        hn = [sb(f"hn_{k}", [P, D]) for k in range(2)]
        ht = [sb(f"ht_{k}", [P, P]) for k in range(2)]
        w1_now = [sb(f"w1_now_{k}", [P, F]) for k in range(2)]
        hid = [sb(f"hid_{k}", [P, FC, P]) for k in range(2)]
        base = [sb(f"base_{k}", [P, D]) for k in range(2)]
        base2 = [sb(f"base2_{k}", [P, D]) for k in range(2)]
        ob = [sb(f"ob_{k}", [P, D]) for k in range(2)]

        def sems(names):
            return [sem(n) for n in names.split()]

        x_in = [sem(f"x_in_{k}") for k in range(STEPS)]
        aw_in, ident_in, const_in, small_in, w1_in, w2_in = sems("aw_in ident_in const_in small_in w1_in w2_in")
        prep_in, prep_mm, prep_ready = sems("prep_in prep_mm prep_ready")
        dve_norm, dve_route, dve_soft = sems("dve_norm dve_route dve_soft")
        x_scalars, xh_ready = sems("x_scalars xh_ready")
        c_done, t_done, u_done, s_done, m_done, g_done, o_done = sems("c_done t_done u_done s_done m_done g_done o_done")
        c_ready, xt_ready, u_ready, m_ready, g_ready = sems("c_ready xt_ready u_ready m_ready g_ready")
        nmax_ready, exp_done, wn_ready = sems("nmax_ready exp_done wn_ready")
        o_read, nlog_ready, eneg_ready = sems("o_read nlog_ready eneg_ready")
        acc_ready, rank_done, slot_ready, alpha_ready = sems("acc_ready rank_done slot_ready alpha_ready")
        stored = sem("stored")
        total_done, fill_ready, table_ready, fill_done = sems("total_done fill_ready table_ready fill_done")
        row_in = [sem(f"row_in_{k}") for k in range(NROW)]
        hn_ready, hnt_done, ht_ready, w1_ready, l1_done = sems("hn_ready hnt_done ht_ready w1_ready l1_done")
        relu_a, relu_b, base_ready, base2_ready, l2_done, ob_ready = sems("relu_a relu_b base_ready base2_ready l2_done ob_ready")
        out_done = [sem(f"out_done_{k}") for k in range(2)]

        block = ctx.enter_context(nc.Block())

        def x_tile(t):
            return x_sb[:, t * D:(t + 1) * D]

        def tiles(s):
            return range(ST * s, ST * (s + 1))

        def expert(eng, b):
            return eng.value_load(blk_exp[0:1, b:b + 1], min_val=0, max_val=E - 1)


        @block.sync
        def _(sp):
            for s in range(STEPS):
                sp.dma_start(x_sb[:, ST * D * s:ST * D * (s + 1)], x[:, 2 * s:2 * s + 2].rearrange("p n a -> p (n a)"))\
                    .then_inc(x_in[s], 16)
            sp.wait_ge(x_in[STEPS - 2], 16)
            sp.dma_start(b1_sb[:], b1).then_inc(w1_in, 16)
            sp.dma_start(w1_sb[:], w1).then_inc(w1_in, 16)
            sp.dma_start(b2_sb[:], b2.partition_broadcast(P)).then_inc(w2_in, 16)
            sp.dma_start(w2_sb[:], w2).then_inc(w2_in, 16)
            sp.wait_ge(const_in, 16 * 5)
            sp.dma_start(scratch[E * CAP:E * CAP + P, :], fill_sb[:]).then_inc(fill_done, 16)
            sp.wait_ge(fill_ready, 1)
            with sp.Fori(0, E) as e:
                r = sp.value_load(fill_row[0:1, bass.ds(e, 1)], min_val=0, max_val=ROWS - P)
                sp.dma_start(scratch[bass.ds(r, P), :], fill_sb[:]).then_inc(fill_done, 16)
            sp.wait_ge(table_ready, 1)
            for b in range(NBLK):
                r = sp.value_load(blk_row[0:1, b:b + 1], min_val=0, max_val=ROWS - P)
                if b == 0:
                    sp.wait_ge(fill_done, 16 * (E + 1))
                    sp.wait_ge(stored, 16 * TILES)
                if b >= NROW:
                    sp.wait_ge(row_in[b % NROW], 16 * (b // NROW))
                sp.dma_start(rin[:, b, :], scratch[bass.ds(r, P), :]).then_inc(row_in[b % NROW], 16)
            sp.wait_ge(out_done[0], 16 * ((NBLK + 1) // 2))
            sp.wait_ge(out_done[1], 16 * (NBLK // 2))

        @block.gpsimd
        def _(pool):
            for n, group in enumerate(GROUPS):
                pool.wait_ge(slot_ready, n + 1)
                pool.wait_ge(alpha_ready, n + 1)
                for s in group:
                    for t in tiles(s):
                        pool.indirect_dma_start(scratch, bass.IndirectOffsetOnAxis(ap=slot[:, t:t + 1], axis=0),
                                                rows[:, t, :], None).then_inc(stored, 16)
            for b in range(NBLK):
                pool.wait_ge(ob_ready, b + 1)
                pool.indirect_dma_start(out, bass.IndirectOffsetOnAxis(ap=rin[:, b, C_TOK:C_TOK + 1].bitcast(U32), axis=0),
                                        ob[b % 2][:], None, bounds_check=TOKENS - 1,
                                        oob_is_err=False).then_inc(out_done[b % 2], 16)

        @block.scalar
        def _(act):
            act.dma_start(aw[:], attn_w).then_inc(aw_in, 16)
            act.dma_start(qb[:], qkv_b).then_inc(small_in, 16)
            act.dma_start(ic[:, 0:D], ident).then_inc(ident_in, 16)
            act.dma_start(pw[:], proj_w).then_inc(small_in, 16)
            act.dma_start(cf[:], const_f).then_inc(const_in, 16)
            act.dma_start(cb[:], const_b).then_inc(const_in, 16)
            act.dma_start(tokid[:], token_ids).then_inc(const_in, 16)
            act.dma_start(tc[:], table_c).then_inc(const_in, 16)
            act.dma_start(fill_sb[:], filler).then_inc(const_in, 16)

            for s in range(STEPS + 2):
                if s < STEPS:
                    act.wait_ge(x_scalars, 1 if s < 2 else 2)
                    if s >= 2:
                        act.wait_ge(t_done, s - 1)
                    for t in tiles(s):
                        last = act.activation(xh[s % 2][:, t - ST * s, :], x_tile(t), ACT.Identity,
                                              bias=hbias[:, t:t + 1], scale=rs1[:, 1, t:t + 1])
                    last.then_inc(xh_ready, 1)
                    act.wait_ge(c_done, s + 1)
                    if s >= 1:
                        act.wait_ge(u_done, s)
                    act.copy(c_sb[:], ps_c[:, 0:2 * D]).then_inc(c_ready, 1)
                if 1 <= s <= STEPS:
                    act.wait_ge(m_done, s)
                    if s >= 2:
                        act.wait_ge(g_done, s - 1)
                    act.copy(m_sb[:], ps_m[:, 0:2 * AW]).then_inc(m_ready, 1)
                if s < STEPS:
                    act.wait_ge(t_done, s + 1)
                    if s >= 2:
                        act.wait_ge(o_done, s - 1)
                    act.copy(xt[s % 2][:], ps_t[:]).then_inc(xt_ready, 1)
                    act.wait_ge(u_done, s + 1)
                    if s >= 1:
                        act.wait_ge(s_done, s)
                    act.copy(u_sb[:], ps_u[:, 0:2 * D]).then_inc(u_ready, 1)
                    act.wait_ge(nmax_ready, s + 1)
                    if s >= 1:
                        act.wait_ge(wn_ready, s)
                    for b in range(2):
                        last = act.activation(w_sb[:, b, :], ps_s[:, b * D:(b + 1) * D], ACT.Exp, bias=nmax[:, b:b + 1],
                                              scale=SCALE, accum_out=den[:, b:b + 1])
                    last.then_inc(exp_done, 1)
                if s - 2 in GROUP_OF:
                    n = GROUP_OF[s - 2]
                    a, z = ST * GROUPS[n][0], ST * (GROUPS[n][-1] + 1)
                    act.wait_ge(nlog_ready, n + 1)
                    act.activation(eneg[:, a:z], nlog[:, a:z], ACT.Exp).then_inc(eneg_ready, 1)

            def turn(b):
                e = expert(act, b)
                weight, bias = aw[:, bass.ds(e + A_G, 1)], aw[:, bass.ds(e + A_B, 1)]
                act.wait_ge(hnt_done, b + 1)
                if b >= 2:
                    act.wait_ge(l1_done, b - 1)
                act.activation(ht[b % 2][:], ps_xt[b % 2][:, 0:P], ACT.Identity, bias=bias, scale=weight).then_inc(ht_ready, 1)
                return e

            act.wait_ge(table_ready, 1)
            act.wait_ge(w1_in, 32)
            e_next = None
            for b in range(-1, NBLK):
                e = e_next
                if b + 1 < NBLK:
                    e_next = turn(b + 1)
                if b < 0:
                    continue
                if b >= 2:
                    act.wait_ge(base2_ready, b - 1)
                act.activation(base[b % 2][:], rin[:, b, 0:D], ACT.Identity, bias=rin[:, b, C_SB:C_SB + 1],
                               scale=rin[:, b, C_SA:C_SA + 1]).then_inc(base_ready, 1)
                act.wait_ge(l1_done, b + 1)
                if b >= 2:
                    act.wait_ge(l2_done, b - 1)
                for c in range(ACT_FC):
                    last = act.activation(hid[b % 2][:, c, :], ps_ha[b % 2][:, c * P:(c + 1) * P], ACT.Relu,
                                          bias=b1_sb[:, bass.ds(e * FC + c, 1)])
                last.then_inc(relu_a, 1)

        @block.vector
        def _(dve):
            norm, route, soft = Chain(dve, dve_norm), Chain(dve, dve_route), Chain(dve, dve_soft)

            def stats1(a, z):
                for s in range(a // ST, z // ST):
                    dve.wait_ge(x_in[s], 16)
                    for t in tiles(s):
                        norm.mark(dve.bn_stats(bn1[:, t, :], x_tile(t)))

            def moments(bn, mom, var, a, z):
                norm.ready()
                dve.tensor_tensor(mom[:, 1, a:z], bn[:, a:z, 2], bn[:, a:z, 5], ALU.add)
                dve.tensor_tensor(mom[:, 0, a:z], bn[:, a:z, 1], bn[:, a:z, 4], ALU.add)
                norm.link(dve.tensor_tensor(mom[:, 2, a:z], bn[:, a:z, 1], bn[:, a:z, 4], ALU.subtract))
                norm.link(dve.scalar_tensor_tensor(out=mom[:, 3, a:z], in0=mom[:, 2, a:z], scalar=0.25,
                                                   in1=mom[:, 2, a:z], op0=ALU.mult, op1=ALU.mult))
                norm.link(dve.scalar_tensor_tensor(out=mom[:, 1, a:z], in0=mom[:, 1, a:z], scalar=1.0 / D,
                                                   in1=mom[:, 3, a:z], op0=ALU.mult, op1=ALU.add))
                dve.tensor_scalar(var[:, 0, a:z], mom[:, 1, a:z], EPS, None, ALU.add)
                norm.link(dve.tensor_scalar(var[:, 1, a:z], mom[:, 1, a:z], 1.0 + EPS, EPS * EPS, ALU.mult, ALU.add))

            def guess(var, rs, nw, a, z):
                half = nw[:, :, a:z].bitcast(I32)
                norm.link(dve.tensor_scalar(half, var[:, :, a:z].bitcast(I32), 1, None, ALU.logical_shift_right))
                norm.link(dve.tensor_scalar(rs[:, :, a:z].bitcast(I32), half, -1.0, MAGIC, ALU.mult, ALU.add))

            def newton(k, var, rs, nw, a, z):
                y, t = rs[:, :, a:z], nw[:, :, a:z]
                if k == 0:
                    ins = dve.tensor_tensor(t, y, y, ALU.mult)
                elif k == 1:
                    ins = dve.scalar_tensor_tensor(out=t, in0=t, scalar=-0.5, in1=var[:, :, a:z], op0=ALU.mult, op1=ALU.mult)
                else:
                    ins = dve.scalar_tensor_tensor(out=y, in0=t, scalar=1.5, in1=y, op0=ALU.add, op1=ALU.mult)
                norm.mark(ins)

            def scalars1(a, z):
                moments(bn1, mom1, var1, a, z)
                guess(var1, rs1, nw1, a, z)
                for k in range(9):
                    newton(k % 3, var1, rs1, nw1, a, z)
                    norm.ready()
                r, rho = rs1[:, 0, a:z], rs1[:, 1, a:z]
                norm.link(dve.scalar_tensor_tensor(out=nw1[:, 0, a:z], in0=mom1[:, 0, a:z], scalar=-0.5, in1=rho,
                                                   op0=ALU.mult, op1=ALU.mult))
                dve.tensor_scalar(hbias[:, a:z], nw1[:, 0, a:z], 1.0, None, ALU.add).then_inc(x_scalars, 1)
                dve.tensor_scalar(xs1[:, a:z], r, 1.0, None, ALU.add)
                dve.scalar_tensor_tensor(out=mr1[:, a:z], in0=mom1[:, 0, a:z], scalar=0.5, in1=r, op0=ALU.mult, op1=ALU.mult)
                norm.link(dve.tensor_tensor(nw1[:, 1, a:z], var1[:, 1, a:z], rho, ALU.mult))
                norm.mark(dve.tensor_tensor(rfac[:, a:z], nw1[:, 1, a:z], xs1[:, a:z], ALU.mult))

            dve.memset(one_d[:], 1.0 / D)
            dve.memset(acc[:, 0, :], 0.0)
            dve.wait_ge(aw_in, 16)
            norm.link(dve.tensor_tensor(nbw[:], aw[:, A_COL + 1:A_COL + 2], aw[:, A_COL:A_COL + 1], ALU.subtract))
            dve.tensor_scalar(nb_t[:], one_d[:], nbw[:], None, ALU.mult)
            dve.tensor_scalar(pb_t[:], one_d[:], aw[:, A_COL + 2:A_COL + 3], None, ALU.mult).then_inc(prep_in, 1)
            dve.tensor_copy(pt[:, 0:D], aw[:, A_P:A_P + D])
            stats1(0, 2 * ST)
            scalars1(0, 2 * ST)
            dve.wait_ge(prep_mm, 2)
            dve.scalar_tensor_tensor(out=wt[:], in0=aw[:, 0:3 * D], scalar=aw[:, A_COL:A_COL + 1], in1=bank[0][:, 0:3 * D],
                                     op0=ALU.mult, op1=ALU.add)
            dve.tensor_tensor(ic[:, D:AW], aw[:, A_C:A_C + E], bank[1][:, 0:E], ALU.subtract).then_inc(prep_in, 1)
            dve.wait_ge(prep_in, 2)
            for b in range(2):
                dve.tensor_copy(g_sb[:, b, AW:OW], ic[:, D:AW])
            dve.wait_ge(prep_mm, 3)
            dve.tensor_copy(wv[:], bank[2][:, 0:D])
            dve.tensor_copy(pbias[:], bank[3][:, 0:AW])
            dve.tensor_copy(pt[:, D:AW], bank[4][:, 0:E]).then_inc(prep_ready, 1)
            stats1(2 * ST, TILES)
            scalars1(2 * ST, TILES)
            dve.wait_ge(prep_ready, 1)
            dve.wait_ge(const_in, 16 * 5)

            def residual(s):
                dve.wait_ge(o_done, s + 1)
                both = bank_o[:, :, 0:2 * OW].rearrange("p b (j c) -> p b j c", j=2)
                a, z = ST * s, ST * (s + 1)
                cut = "p (b j) c -> p b j c"
                fac = rfac[:, a:z].rearrange("p (b j) -> p b j", b=2).unsqueeze(3).to_broadcast([P, 2, 2, E])
                route.mark(dve.tensor_tensor(aff0[:, a:z, :].rearrange(cut, b=2), both[:, :, :, AW:OW], fac, ALU.mult))
                for t in tiles(s):
                    k = t - a
                    norm.mark(dve.scalar_tensor_tensor(out=rows[:, t, 0:D], in0=x_tile(t), scalar=xs1[:, t:t + 1],
                                                       in1=bank_o[:, k // 2, (k % 2) * OW:(k % 2) * OW + D],
                                                       op0=ALU.mult, op1=ALU.add))
                route.ready()
                dve.tensor_tensor(aff[:, a:z, :].rearrange(cut, b=2), both[:, :, :, D:AW],
                                  aff0[:, a:z, :].rearrange(cut, b=2), ALU.add).then_inc(o_read, 1)
                dve.tensor_copy(rows[:, a:z, C_TOK].bitcast(I32), tokid[:, a:z])
                norm.ready()
                for t in tiles(s):
                    norm.mark(dve.bn_stats(bn2[:, t, :], rows[:, t, 0:D]))

            def route_group(n):
                a, z = ST * GROUPS[n][0], ST * (GROUPS[n][-1] + 1)
                w = z - a
                desc = cf[:, K_DESC:K_DESC + w * E].rearrange("p (t e) -> p t e", t=w)

                def wide(v):
                    return v[:, a:z].unsqueeze(2).to_broadcast([P, w, E])

                dve.wait_ge(o_read, GROUPS[n][-1] + 1)
                route.mark(dve.tensor_reduce(amax[:, a:z], aff[:, a:z, :], AX.X, ALU.max))
                norm.ready()
                dve.tensor_tensor(mom2[:, 1, a:z], bn2[:, a:z, 2], bn2[:, a:z, 5], ALU.add)
                norm.mark(dve.tensor_tensor(mom2[:, 2, a:z], bn2[:, a:z, 1], bn2[:, a:z, 4], ALU.subtract))
                route.ready()
                route.mark(dve.tensor_tensor(hit[:, a:z, :], aff[:, a:z, :], wide(amax), ALU.is_equal))
                norm.ready()
                norm.mark(dve.scalar_tensor_tensor(out=mom2[:, 3, a:z], in0=mom2[:, 2, a:z], scalar=0.25,
                                                   in1=mom2[:, 2, a:z], op0=ALU.mult, op1=ALU.mult))
                dve.tensor_tensor(mom2[:, 0, a:z], bn2[:, a:z, 1], bn2[:, a:z, 4], ALU.add)
                route.ready()
                route.mark(dve.tensor_tensor(val[:, a:z, :], hit[:, a:z, :], desc, ALU.mult))
                norm.ready()
                norm.mark(dve.scalar_tensor_tensor(out=mom2[:, 1, a:z], in0=mom2[:, 1, a:z], scalar=1.0 / D,
                                                   in1=mom2[:, 3, a:z], op0=ALU.mult, op1=ALU.add))
                route.ready()
                route.mark(dve.tensor_reduce(first[:, a:z], val[:, a:z, :], AX.X, ALU.max))
                norm.ready()
                dve.tensor_scalar(var2[:, 0, a:z], mom2[:, 1, a:z], EPS, None, ALU.add)
                norm.mark(dve.tensor_scalar(var2[:, 1, a:z], mom2[:, 1, a:z], 1.0 + EPS, EPS * EPS, ALU.mult, ALU.add))
                route.ready()
                route.mark(dve.tensor_tensor(onehot[:, a:z, :], desc, wide(first), ALU.is_equal))
                norm.ready()
                half = nw2[:, :, a:z].bitcast(I32)
                norm.mark(dve.tensor_scalar(half, var2[:, :, a:z].bitcast(I32), 1, None, ALU.logical_shift_right))
                route.ready()
                route.mark(dve.tensor_reduce(osum[:, n, :], onehot[:, a:z, :].rearrange("p t e -> p e t"), AX.X, ALU.add))
                norm.ready()
                norm.mark(dve.tensor_scalar(rs2[:, :, a:z].bitcast(I32), half, -1.0, MAGIC, ALU.mult, ALU.add))
                route.ready()
                if n >= 1:
                    dve.wait_ge(acc_ready, n)
                dve.tensor_tensor(acc[:, n + 1, :], acc[:, n, :], osum[:, n, :], ALU.add).then_inc(acc_ready, 1)
                for k in range(9):
                    norm.ready()
                    newton(k % 3, var2, rs2, nw2, a, z)
                norm.ready()
                r3, rh = rs2[:, 0, a:z], rs2[:, 1, a:z]
                dve.scalar_tensor_tensor(out=nlog[:, a:z], in0=r3, scalar=-1.0, in1=amax[:, a:z], op0=ALU.mult,
                                         op1=ALU.mult).then_inc(nlog_ready, 1)
                norm.mark(dve.scalar_tensor_tensor(out=msb[:, a:z], in0=mom2[:, 0, a:z], scalar=-0.5, in1=r3,
                                                   op0=ALU.mult, op1=ALU.mult))
                dve.tensor_copy(rows[:, a:z, C_HA], rh)
                dve.scalar_tensor_tensor(out=rows[:, a:z, C_HB], in0=mom2[:, 0, a:z], scalar=-0.5, in1=rh,
                                         op0=ALU.mult, op1=ALU.mult)
                dve.tensor_scalar(rows[:, a:z, C_SA], r3, 1.0, None, ALU.add)
                norm.ready()
                dve.tensor_tensor(rows[:, a:z, C_SB], msb[:, a:z], mr1[:, a:z], ALU.subtract)

            def places(n):
                a, z = ST * GROUPS[n][0], ST * (GROUPS[n][-1] + 1)
                w = z - a
                dve.wait_ge(rank_done, n + 1)
                ecap = cf[:, K_ECAP:K_ECAP + w * E]
                route.mark(dve.tensor_tensor(pos[:, a:z, :].rearrange("p t e -> p (t e)"), ps_rank[:, 0:w * E], ecap, ALU.add))
                route.ready()
                route.mark(dve.tensor_tensor(posh[:, a:z, :], pos[:, a:z, :], onehot[:, a:z, :], ALU.mult))
                route.ready()
                route.mark(dve.tensor_reduce(posf[:, a:z], posh[:, a:z, :], AX.X, ALU.add))
                route.ready()
                dve.tensor_copy(slot[:, a:z], posf[:, a:z]).then_inc(slot_ready, 1)

            def gates(n):
                a, z = ST * GROUPS[n][0], ST * (GROUPS[n][-1] + 1)
                dve.wait_ge(eneg_ready, n + 1)
                norm.link(dve.tensor_scalar(epos[:, a:z], eneg[:, a:z], 1.0, None, ALU.add))
                dve.reciprocal(rows[:, a:z, C_AL], epos[:, a:z]).then_inc(alpha_ready, 1)

            for s in range(STEPS + 2):
                if 1 <= s <= STEPS:
                    dve.wait_ge(g_done, s)
                    if s >= 2:
                        dve.wait_ge(o_done, s - 1)
                    dve.tensor_tensor(g_sb[:, :, 0:AW], ps_g[:, 0:2 * AW].rearrange("p (b c) -> p b c", b=2),
                                      pbias[:].unsqueeze(1).to_broadcast([P, 2, AW]), ALU.add).then_inc(g_ready, 1)
                if s < STEPS:
                    dve.wait_ge(s_done, s + 1)
                    soft.link(dve.tensor_reduce(smax[:], ps_s[:, 0:2 * D].rearrange("p (b k) -> p b k", b=2), AX.X, ALU.max))
                    dve.tensor_scalar(nmax[:], smax[:], -SCALE, None, ALU.mult).then_inc(nmax_ready, 1)
                if s - 2 in GROUP_OF:
                    places(GROUP_OF[s - 2])
                if s < STEPS:
                    dve.wait_ge(exp_done, s + 1)
                    soft.link(dve.reciprocal(rden[:], den[:]))
                    if s >= 1:
                        dve.wait_ge(m_done, s)
                    for b in range(2):
                        last = dve.tensor_scalar(wn_sb[:, b, :], w_sb[:, b, :], rden[:, b:b + 1], None, ALU.mult)
                    last.then_inc(wn_ready, 1)
                if s - 2 in GROUP_OF:
                    gates(GROUP_OF[s - 2])
                if 1 <= s <= STEPS:
                    residual(s - 1)
                    if s - 1 in GROUP_OF:
                        route_group(GROUP_OF[s - 1])

            dve.wait_ge(total_done, 1)
            link = route.link
            link(dve.tensor_copy(cnt[:], bank[0][0:1, 0:E]))
            link(dve.tensor_tensor(frow_f[:], cnt[:], tc[:, T_ECAP:T_ECAP + E], ALU.add))
            dve.tensor_copy(fill_row[:], frow_f[:]).then_inc(fill_ready, 1)
            thr = tc[:, T_THR:T_THR + E * TILES].rearrange("p (e j) -> p e j", e=E)
            link(dve.tensor_tensor(over[:], cnt[:].unsqueeze(2).to_broadcast([1, E, TILES]), thr, ALU.is_gt))
            link(dve.tensor_reduce(nblk[:], over[:], AX.X, ALU.add))
            lower = tc[:, T_LOW:T_LOW + E * E].rearrange("p (e j) -> p e j", e=E)
            link(dve.tensor_tensor(low[:], nblk[:].unsqueeze(1).to_broadcast([1, E, E]), lower, ALU.mult))
            link(dve.tensor_reduce(cum[:], low[:], AX.X, ALU.add))
            blk = tc[:, T_BLK:T_BLK + NBLK * E].rearrange("p (b e) -> p b e", b=NBLK)
            link(dve.tensor_tensor(past[:], blk, cum[:].unsqueeze(1).to_broadcast([1, NBLK, E]), ALU.is_ge))
            link(dve.tensor_tensor(pastn[:], past[:], nblk[:].unsqueeze(1).to_broadcast([1, NBLK, E]), ALU.mult))
            dve.tensor_reduce(bex[:], past[:], AX.X, ALU.add)
            link(dve.tensor_reduce(bcum[:], pastn[:], AX.X, ALU.add))
            link(dve.scalar_tensor_tensor(out=bst[:], in0=bcum[:], scalar=-float(P), in1=tc[:, T_B128:T_B128 + NBLK],
                                          op0=ALU.mult, op1=ALU.add))
            link(dve.scalar_tensor_tensor(out=bst2[:], in0=bex[:], scalar=float(CAP), in1=bst[:], op0=ALU.mult, op1=ALU.add))
            dve.tensor_scalar(blk_row[:], bst2[:], float(E * CAP), None, ALU.min)
            dve.tensor_scalar(blk_exp[:], bex[:], float(E - 1), None, ALU.min).then_inc(table_ready, 1)

            def whiten(b):
                dve.wait_ge(row_in[b % NROW], 16 * (b // NROW + 1))
                if b >= 2:
                    dve.wait_ge(hnt_done, b - 1)
                dve.tensor_scalar(hn[b % 2][:], rin[:, b, 0:D], rin[:, b, C_HA:C_HA + 1], rin[:, b, C_HB:C_HB + 1],
                                  ALU.mult, ALU.add).then_inc(hn_ready, 1)

            def fetch_w1(b):
                e = expert(dve, b)
                src = w1_sb[:, bass.ds(e * F, F)]
                if b >= 2:
                    dve.wait_ge(l1_done, b - 1)
                dve.tensor_copy(w1_now[b % 2][:], src).then_inc(w1_ready, 1)
                return e

            dve.wait_ge(w1_in, 32)
            dve.wait_ge(w2_in, 32)
            dve.wait_ge(table_ready, 1)
            e_next = fetch_w1(0)
            whiten(0)
            whiten(1)
            for b in range(NBLK + 1):
                e = e_next
                if b < NBLK:
                    if b + 1 < NBLK:
                        e_next = fetch_w1(b + 1)
                    if b + 2 < NBLK:
                        whiten(b + 2)
                    biases = [b1_sb[:, bass.ds(e * FC + c, 1)] for c in range(ACT_FC, FC)]
                    add = b2_sb[:, bass.ds(e * D, D)]
                    dve.wait_ge(l1_done, b + 1)
                    if b >= 2:
                        dve.wait_ge(l2_done, b - 1)
                    for c in range(ACT_FC, FC):
                        k = c - ACT_FC
                        last = dve.tensor_scalar(hid[b % 2][:, c, :], ps_hb[b % 2][:, k * P:(k + 1) * P],
                                                 biases[k], 0.0, ALU.add, ALU.max)
                    last.then_inc(relu_b, 1)
                    dve.wait_ge(base_ready, b + 1)
                    if b >= 2:
                        dve.wait_ge(ob_ready, b - 1)
                    dve.scalar_tensor_tensor(out=base2[b % 2][:], in0=add, scalar=rin[:, b, C_AL:C_AL + 1],
                                             in1=base[b % 2][:], op0=ALU.mult, op1=ALU.add).then_inc(base2_ready, 1)
                if b >= 1:
                    q = b - 1
                    dve.wait_ge(l2_done, q + 1)
                    dve.wait_ge(base2_ready, q + 1)
                    if q >= 2:
                        dve.wait_ge(out_done[q % 2], 16 * (q // 2))
                    dve.scalar_tensor_tensor(out=ob[q % 2][:], in0=ps_y[q % 2][:, 0:D], scalar=rin[:, q, C_AL:C_AL + 1],
                                             in1=base2[q % 2][:], op0=ALU.mult, op1=ALU.add).then_inc(ob_ready, 1)

        @block.tensor
        def _(pe):
            def mm(out, lhs, rhs, start=True, stop=True):
                return pe.matmul(out, lhs, rhs, start=start, stop=stop)

            pe.wait_ge(prep_in, 1)
            pe.wait_ge(small_in, 32)
            mm(bank[0][:, 0:3 * D], nb_t[:], aw[:, 0:3 * D], stop=False)
            mm(bank[0][:, 0:3 * D], one_d[0:1, :], qb[:], start=False).then_inc(prep_mm, 1)
            mm(bank[1][:, 0:E], one_d[:], aw[:, A_C:A_C + E]).then_inc(prep_mm, 1)
            pe.wait_ge(ident_in, 16)
            pe.wait_ge(prep_in, 2)
            pe.transpose(bank[2][:, 0:D], wt[:, 2 * D:3 * D], idt)
            mm(bank[3][:, 0:AW], pb_t[:], ic[:])
            mm(bank[4][:, 0:E], pw[:], ic[:, D:AW]).then_inc(prep_mm, 1)
            pe.wait_ge(prep_ready, 1)
            pe.wait_ge(const_in, 16 * 5)

            for s in range(STEPS + 2):
                if s < STEPS:
                    pe.wait_ge(xh_ready, s + 1)
                    if s >= 1:
                        pe.wait_ge(c_ready, s)
                    for b in range(2):
                        for j in range(2):
                            h = xh[s % 2][:, 2 * b + j, :]
                            last = mm(ps_c[:, b * D:(b + 1) * D], h, h, start=(j == 0), stop=(j == 1))
                    last.then_inc(c_done, 1)
                if 1 <= s <= STEPS:
                    pe.wait_ge(wn_ready, s)
                    if s >= 2:
                        pe.wait_ge(m_ready, s - 1)
                    for b in range(2):
                        last = mm(ps_m[:, b * AW:(b + 1) * AW], wn_sb[:, b, :], pt[:])
                    last.then_inc(m_done, 1)
                if s < STEPS:
                    if s >= 1:
                        pe.wait_ge(xt_ready, s)
                    for k in range(ST):
                        last = pe.transpose(ps_t[:, k * P:(k + 1) * P], xh[s % 2][:, k, :], idt)
                    last.then_inc(t_done, 1)
                    pe.wait_ge(c_ready, s + 1)
                    if s >= 1:
                        pe.wait_ge(u_ready, s)
                    for b in range(2):
                        last = mm(ps_u[:, b * D:(b + 1) * D], c_sb[:, b * D:(b + 1) * D], wk_t)
                    last.then_inc(u_done, 1)
                if 1 <= s <= STEPS:
                    pe.wait_ge(m_ready, s)
                    if s >= 2:
                        pe.wait_ge(g_ready, s - 1)
                    if s >= 3 and s - 3 in GROUP_OF:
                        pe.wait_ge(slot_ready, GROUP_OF[s - 3] + 1)
                    mm(ps_g[:, 0:2 * AW], wv[:], m_sb[:]).then_inc(g_done, 1)
                if s < STEPS:
                    pe.wait_ge(u_ready, s + 1)
                    if s >= 1:
                        pe.wait_ge(exp_done, s)
                    mm(ps_s[:, 0:2 * D], wq_t, u_sb[:]).then_inc(s_done, 1)
                if s - 2 in GROUP_OF:
                    n = GROUP_OF[s - 2]
                    a, z = ST * GROUPS[n][0], ST * (GROUPS[n][-1] + 1)
                    w = z - a
                    oh = onehot[:, a:z, :].rearrange("p t e -> p (t e)")
                    pe.wait_ge(acc_ready, n + 1)
                    if s <= STEPS:
                        pe.wait_ge(g_ready, s)
                    mm(ps_rank[:, 0:w * E], tri, oh, stop=False)
                    for t in range(1, w):
                        mm(ps_rank[:, t * E:w * E], ones_b, oh[:, 0:(w - t) * E], start=False, stop=False)
                    mm(ps_rank[:, 0:w * E], ones_b, acc[:, n, :].unsqueeze(1).to_broadcast([P, w, E]),
                       start=False).then_inc(rank_done, 1)
                if 1 <= s <= STEPS:
                    pe.wait_ge(g_ready, s)
                    pe.wait_ge(xt_ready, s)
                    if s >= 2:
                        pe.wait_ge(o_read, s - 1)
                    for k in range(ST):
                        last = mm(bank_o[:, k // 2, (k % 2) * OW:(k % 2 + 1) * OW], xt[(s - 1) % 2][:, k * P:(k + 1) * P],
                                  g_sb[:, k // 2, :])
                    last.then_inc(o_done, 1)
                if s == STEPS:
                    pe.wait_ge(acc_ready, len(GROUPS))
                    mm(bank[0][:, 0:E], ones_b, acc[:, len(GROUPS), :]).then_inc(total_done, 1)

            def turn(b):
                pe.wait_ge(hn_ready, b + 1)
                if b >= 2:
                    pe.wait_ge(ht_ready, b - 1)
                pe.transpose(ps_xt[b % 2][:, 0:P], hn[b % 2][:], idt).then_inc(hnt_done, 1)

            pe.wait_ge(table_ready, 1)
            pe.wait_ge(w2_in, 32)
            turn(0)
            e = None
            for b in range(NBLK + 1):
                e_last = e
                if b < NBLK:
                    e = expert(pe, b)
                    if b + 1 < NBLK:
                        turn(b + 1)
                    pe.wait_ge(ht_ready, b + 1)
                    pe.wait_ge(w1_ready, b + 1)
                    if b >= 2:
                        pe.wait_ge(relu_a, b - 1)
                        pe.wait_ge(relu_b, b - 1)
                    for c in range(FC):
                        half, k = (ps_ha, c) if c < ACT_FC else (ps_hb, c - ACT_FC)
                        last = mm(half[b % 2][:, k * P:(k + 1) * P], w1_now[b % 2][:, c * P:(c + 1) * P], ht[b % 2][:])
                    last.then_inc(l1_done, 1)
                if b >= 1:
                    q = b - 1
                    second = [w2_sb[:, bass.ds((e_last * FC + c) * D, D)] for c in range(FC)]
                    pe.wait_ge(relu_a, q + 1)
                    pe.wait_ge(relu_b, q + 1)
                    if q >= 2:
                        pe.wait_ge(ob_ready, q - 1)
                    for c in range(FC):
                        last = mm(ps_y[q % 2][:, 0:D], hid[q % 2][:, c, :], second[c], start=(c == 0), stop=(c == FC - 1))
                    last.then_inc(l2_done, 1)


def kernel(L0_attn_x, L0_attn_norm_w, L0_attn_norm_b, L0_attn_qkv_w, L0_attn_qkv_b, L0_attn_proj_w, L0_attn_proj_b,
           L0_ffn_centroids, L0_ffn_ln_g, L0_ffn_ln_b, L0_ffn_w1, L0_ffn_b1, L0_ffn_w2, L0_ffn_b2):
    import concourse.bacc as bacc
    from concourse.bass_utils import run_bass_kernel_spmd

    f = np.float32
    attn_w = np.concatenate(
        [L0_attn_qkv_w.T, L0_attn_proj_w.T, L0_ffn_centroids.T, L0_ffn_ln_g.T, L0_ffn_ln_b.T,
         L0_attn_norm_w[:, None], L0_attn_norm_b[:, None], L0_attn_proj_b[:, None]], axis=1)
    arrays = {
        "x": np.reshape(L0_attn_x, (B, P, 2, D)).transpose(1, 0, 2, 3).reshape(P, B, 2 * D),
        "attn_w": attn_w,
        "proj_w": L0_attn_proj_w,
        "qkv_b": L0_attn_qkv_b[None, :],
        "w1": L0_ffn_w1.transpose(2, 0, 1).reshape(D, E * F),
        "w2": L0_ffn_w2.reshape(E, D, FC, P).transpose(3, 0, 2, 1).reshape(P, E * FC * D),
        "b1": L0_ffn_b1.reshape(E * FC, P).T,
        "b2": L0_ffn_b2.reshape(E * D),
    }
    import ml_dtypes
    eight = np.arange(E)
    const_f = np.zeros((P, K_END), f)
    const_f[:, K_DESC:K_DESC + WMAX * E] = np.tile(E - eight, WMAX)
    const_f[:, K_ECAP:K_ECAP + WMAX * E] = np.tile(eight * CAP, WMAX)
    p, m = np.arange(P)[:, None], np.arange(P)[None, :]
    const_b = np.concatenate([p < m, np.ones((P, P))], axis=1).astype(ml_dtypes.bfloat16)
    tile = np.arange(TILES)[None, :]
    filler = np.zeros((P, RW), np.int32)
    filler[:, C_TOK] = NO_TOKEN
    table = np.zeros((1, T_END), f)
    table[0, T_BLK:T_BLK + NBLK * E] = np.repeat(np.arange(NBLK), E)
    table[0, T_THR:T_THR + E * TILES] = np.tile(np.arange(TILES) * P, E)
    table[0, T_LOW:T_LOW + E * E] = (eight[None, :] <= eight[:, None]).reshape(-1)
    table[0, T_B128:T_B128 + NBLK] = np.arange(NBLK) * P
    table[0, T_ECAP:T_ECAP + E] = eight * CAP
    arrays.update({
        "const_f": const_f, "const_b": const_b, "ident": np.eye(P, dtype=f),
        "token_ids": (tile // 2 * L + 2 * p + tile % 2).astype(np.int32),
        "table_c": table, "filler": filler.view(f),
    })
    nc = bacc.Bacc("TRN2", target_bir_lowering=False, num_devices=1)
    feed, args = {}, []
    for name, a in arrays.items():
        a = np.ascontiguousarray(a)
        feed[f"in_{name}"] = a
        args.append(nc.dram_tensor(f"in_{name}", a.shape, mybir.dt.from_np(a.dtype), kind="ExternalInput").ap())
    args.append(nc.dram_tensor("out", (TOKENS, D), F32, kind="ExternalOutput").ap())
    build(nc, *args)
    r = run_bass_kernel_spmd(nc, [feed], core_ids=[0])
    return np.reshape(r.results[0]["out"], (B, L, D))
```

```python
from contextlib import ExitStack

import numpy as np

import concourse.bass as bass
from concourse import mybir

P = 128
D = 128
B, L = 16, 256
TOKENS = B * L
E, F = 8, 512
FC = F // P
TILES = TOKENS // P
ST = 4
STEPS = TILES // ST
AW = D + E
OW = AW + E
EPS = 1e-5
SCALE = 1.0 / 16.0
NBLK = TILES + E - 1
CAP = TOKENS + P
ROWS = E * CAP + P
C_HA, C_HB, C_SA, C_SB, C_AL, C_TOK = D, D + 1, D + 2, D + 3, D + 4, D + 5
RW = D + 6
NO_TOKEN = 1 << 20
ACT_CHUNKS = (3, 2)
TAIL_FULL = 5
ACT_GATE, POOL_LAST = 4, 2
NOB = 8
NROW = 4

ALU = mybir.AluOpType
ACT = mybir.ActivationFunctionType
AX = mybir.AxisListType
F32 = mybir.dt.float32
BF16 = mybir.dt.bfloat16
I32 = mybir.dt.int32
U32 = mybir.dt.uint32

A_W, A_P, A_C, A_G, A_B, A_COL = 0, 384, 512, 520, 528, 536
A_END = 539
T_BLK = 0
T_THR = T_BLK + NBLK * E
T_FULL = T_THR + E * TILES
T_LOW = T_FULL + E * TILES
T_B128 = T_LOW + E * E
T_ECAP = T_B128 + NBLK
T_CAP = T_ECAP + E
T_END = T_CAP + E


GROUPS = [(0, 1), (2, 3), (4,), (5,), (6, 7)]
EARLY = 3
EARLY_TILES = ST * (GROUPS[EARLY - 1][-1] + 1)
NB1 = -(-(EARLY_TILES * P - E * (P - 1)) // P)
NB2 = NBLK - NB1
PARTS = (NBLK - 4, NBLK - 2, NBLK)
ROUND_OF = {EARLY - 1: 0, len(GROUPS) - 1: 1}
LN1 = [(0, 2 * ST), (2 * ST, 4 * ST), (4 * ST, TILES)]
LN1_BEFORE = 11
PREP_STEP = 8
GROUP_OF = {g[-1]: n for n, g in enumerate(GROUPS)}
WMAX = ST * max(len(g) for g in GROUPS)
K_END = WMAX * E

MAGIC = float(0x5F3759DF)
ROOT = 10


class Chain:

    def __init__(self, eng, sem):
        self.eng, self.sem, self.count = eng, sem, 0

    def mark(self, ins):
        self.count += 1
        ins.then_inc(self.sem, 1)

    def ready(self):
        if self.count:
            self.eng.wait_ge(self.sem, self.count)

    def link(self, ins):
        self.mark(ins)
        self.ready()


def build(nc, x, attn_w, proj_w, qkv_b, w1, w2, b1, b2, const_f, const_b, ident, token_ids, table_c, filler, out):
    with ExitStack() as ctx:
        def sb(name, shape, dt=F32):
            return ctx.enter_context(nc.sbuf_tensor(name, shape, dt))

        def sem(name):
            return ctx.enter_context(nc.semaphore(name))

        scratch = nc.dram_tensor("rows_by_expert", [ROWS, RW], F32, kind="Internal").ap()

        bank = [ctx.enter_context(nc.psum_tensor(f"bank{k}", [P, 512], F32)) for k in range(6)]
        bank_o = ctx.enter_context(nc.psum_tensor("bank_o", [P, 2, 512], F32))
        ps_t, ps_c, ps_u, ps_s, ps_m, ps_g = bank
        ps_rank, ps_cnt = ps_g[:, 288:288 + WMAX * E], ps_g[:, 480:480 + E]
        ps_xt = [bank[0], bank[1]]
        ps_ha = [bank[2], bank[3]]
        ps_hb = [bank[4], bank[5]]
        ps_y = [bank_o[:, 0, :], bank_o[:, 1, :]]
        ps_rank_last, ps_cnt_last = bank_o[:, 1, 288:288 + WMAX * E], bank_o[:, 1, 480:480 + E]

        x_sb = sb("x_sb", [P, TILES * D])
        aw = sb("aw", [P, A_END])
        pw = sb("pw", [P, D])
        qb = sb("qb", [1, 3 * D])
        w1_sb = sb("w1_sb", [P, E * F])
        w2_sb = sb("w2_sb", [P, E * FC * D])
        b1_sb = sb("b1_sb", [P, E * FC])
        b2_sb = sb("b2_sb", [P, E * D])
        cf = sb("cf", [P, K_END])
        cb = sb("cb", [P, 2 * P + WMAX * E], BF16)
        tokid = sb("tokid", [P, TILES], I32)
        tc = sb("tc", [1, T_END])
        fill_sb = sb("fill_sb", [P, RW])
        tri, ones_b, begins = cb[:, 0:P], cb[:, P:2 * P], cb[0:1, 2 * P:]

        one_d = sb("one_d", [P, P])
        nbw = sb("nbw", [P, 1])
        nb_t = sb("nb_t", [P, P])
        pb_t = sb("pb_t", [P, P])
        wt = sb("wt", [P, 3 * D])
        wv = sb("wv", [P, D])
        ic = sb("ic", [P, AW])
        pt = sb("pt", [P, AW])
        pb_row = sb("pb_row", [1, 2, AW])
        wq_s = sb("wq_s", [P, D])
        wk_t = wt[:, D:2 * D]
        idt = ic[:, 0:D]

        bn1 = sb("bn1", [P, TILES, 6])
        mom1 = sb("mom1", [P, 4, TILES])
        var1 = sb("var1", [P, 2, TILES])
        rs1 = sb("rs1", [P, 2, TILES])
        nw1 = sb("nw1", [P, 2, TILES])
        hbias = sb("hbias", [P, TILES])
        xs1 = sb("xs1", [P, TILES])
        mr1 = sb("mr1", [P, TILES])
        rfac = sb("rfac", [P, TILES])

        xh = [sb(f"xh_{k}", [P, ST, D]) for k in range(2)]
        xt = [sb(f"xt_{k}", [P, ST * D]) for k in range(2)]
        c_sb = sb("c_sb", [P, 2 * D])
        u_sb = sb("u_sb", [P, 2 * D])
        w_sb = sb("w_sb", [P, 2, D])
        wn_sb = sb("wn_sb", [P, 2, D])
        m_sb = sb("m_sb", [P, 2 * AW])
        g_sb = sb("g_sb", [P, 2, OW])
        nmax = sb("nmax", [P, 2])
        den = sb("den", [P, 2])
        rden = sb("rden", [P, 2])

        rows = sb("rows", [P, TILES, RW])
        bn2 = sb("bn2", [P, TILES, 6])
        mom2 = sb("mom2", [P, 4, TILES])
        var2 = sb("var2", [P, 2, TILES])
        rs2 = sb("rs2", [P, 2, TILES])
        nw2 = sb("nw2", [P, 2, TILES])
        msb = sb("msb", [P, TILES])
        nlog = sb("nlog", [P, TILES])
        eneg = sb("eneg", [P, TILES])
        epos = sb("epos", [P, TILES])
        aff0 = sb("aff0", [P, TILES, E])
        aff = sb("aff", [P, TILES, E])
        amax = sb("amax", [P, TILES])
        hit = sb("hit", [P, TILES, E])
        val = sb("val", [P, TILES, E])
        first = sb("first", [P, TILES])
        onehot = sb("onehot", [P, TILES, E], BF16)
        osum = sb("osum", [P, len(GROUPS), E])
        acc = sb("acc", [P, len(GROUPS) + 1, E], BF16)
        posh = sb("posh", [P, TILES, E])
        posf = sb("posf", [P, TILES])
        slot = sb("slot", [P, TILES], U32)

        cnt = sb("cnt", [1, 2, E])
        over = sb("over", [1, 2, E, TILES])
        nall = sb("nall", [1, E])
        nblk = sb("nblk", [1, 2, E])
        low = sb("low", [1, 2, E, E])
        cum = sb("cum", [1, 2, E])
        cumx = sb("cumx", [1, E])
        done = sb("done", [1, E + 1])
        gap = sb("gap", [1, E])
        ofs = sb("ofs", [1, NB2])
        jump = sb("jump", [1, 2, E])
        past = sb("past", [1, 2, NBLK, E])
        pastj = sb("pastj", [1, 2, NBLK, E])
        bex = sb("bex", [1, NBLK])
        bjump = sb("bjump", [1, NBLK])
        bst = sb("bst", [1, NBLK])
        frow_f = sb("frow_f", [1, E])
        fill_row = sb("fill_row", [1, E], I32)
        blk_row = sb("blk_row", [1, NBLK], I32)
        blk_exp = sb("blk_exp", [1, NBLK], I32)

        rin = sb("rin", [P, NBLK, RW])
        hn = [sb(f"hn_{k}", [P, D]) for k in range(2)]
        ht = [sb(f"ht_{k}", [P, P]) for k in range(2)]
        w1_now = [sb(f"w1_now_{k}", [P, F]) for k in range(2)]
        hid = [sb(f"hid_{k}", [P, FC, P]) for k in range(2)]
        base = [sb(f"base_{k}", [P, D]) for k in range(2)]
        base2 = [sb(f"base2_{k}", [P, D]) for k in range(2)]
        ob = [sb(f"ob_{k}", [P, D]) for k in range(NOB)]

        def sems(names):
            return [sem(n) for n in names.split()]

        x_in = [sem(f"x_in_{k}") for k in range(STEPS)]
        aw_in, ident_in, const_in, small_in, w1_in, w2_in = sems("aw_in ident_in const_in small_in w1_in w2_in")
        prep_in, prep_mm, wt_ready, prep_ready = sems("prep_in prep_mm wt_ready prep_ready")
        dve_norm, dve_stat, dve_route = sems("dve_norm dve_stat dve_route")
        dve_soft, dve_table = sems("dve_soft dve_table")
        x_scalars, xh_ready = sems("x_scalars xh_ready")
        c_done, t_done, u_done, s_done, m_done, g_done, o_done = sems("c_done t_done u_done s_done m_done g_done o_done")
        c_ready, xt_ready, u_ready, m_ready, g_ready = sems("c_ready xt_ready u_ready m_ready g_ready")
        nmax_ready, exp_done, wn_ready = sems("nmax_ready exp_done wn_ready")
        o_read, nlog_ready, eneg_ready = sems("o_read nlog_ready eneg_ready")
        acc_ready, rank_done, slot_ready, alpha_ready = sems("acc_ready rank_done slot_ready alpha_ready")
        stored = [sem("stored_early"), sem("stored_late")]
        fill_ready, table_ready, fill_done = sems("fill_ready table_ready fill_done")
        row_in = [sem(f"row_in_{k}") for k in range(NROW)]
        hn_ready, hnt_done, ht_ready, w1_ready, l1_done = sems("hn_ready hnt_done ht_ready w1_ready l1_done")
        relu_a, relu_b, base_ready, base2_ready, l2_done, ob_ready = sems("relu_a relu_b base_ready base2_ready l2_done ob_ready")
        out_done = [sem(f"out_done_{k}") for k in range(NOB)]

        block = ctx.enter_context(nc.Block())

        def x_tile(t):
            return x_sb[:, t * D:(t + 1) * D]

        def tiles(s):
            return range(ST * s, ST * (s + 1))

        def act_chunks(b):
            return ACT_CHUNKS[b >= NB1]

        def expert(eng, b):
            return eng.value_load(blk_exp[0:1, b:b + 1], min_val=0, max_val=E - 1)

        def further_parts(eng, run, part=0):
            if part + 1 < len(PARTS):
                b = PARTS[part]
                row = eng.value_load(blk_row[0:1, b:b + 1], min_val=0, max_val=ROWS - P)
                with eng.If(row < E * CAP):
                    run(b, PARTS[part + 1])
                    further_parts(eng, run, part + 1)


        @block.sync
        def _(sp):
            for s in range(STEPS):
                sp.dma_start(x_sb[:, ST * D * s:ST * D * (s + 1)], x[:, 2 * s:2 * s + 2].rearrange("p n a -> p (n a)"))\
                    .then_inc(x_in[s], 16)
            sp.wait_ge(x_in[STEPS - 2], 16)
            sp.dma_start(b1_sb[:], b1).then_inc(w1_in, 16)
            sp.dma_start(w1_sb[:], w1).then_inc(w1_in, 16)
            sp.dma_start(b2_sb[:], b2.partition_broadcast(P)).then_inc(w2_in, 16)
            sp.dma_start(w2_sb[:], w2).then_inc(w2_in, 16)
            sp.wait_ge(const_in, 16 * 5)
            sp.dma_start(scratch[E * CAP:E * CAP + P, :], fill_sb[:]).then_inc(fill_done, 16)

            def load(b):
                r = sp.value_load(blk_row[0:1, b:b + 1], min_val=0, max_val=ROWS - P)
                if b >= NROW:
                    sp.wait_ge(row_in[b % NROW], 16 * (b // NROW))
                sp.dma_start(rin[:, b, :], scratch[bass.ds(r, P), :]).then_inc(row_in[b % NROW], 16)

            sp.wait_ge(table_ready, 1)
            sp.wait_ge(stored[0], 16 * EARLY_TILES)
            for b in range(NB1):
                load(b)
            sp.wait_ge(fill_ready, 1)
            for e in range(E):
                r = sp.value_load(fill_row[0:1, e:e + 1], min_val=0, max_val=ROWS - P)
                sp.dma_start(scratch[bass.ds(r, P), :], fill_sb[:]).then_inc(fill_done, 16)
            sp.wait_ge(table_ready, 2)
            sp.wait_ge(fill_done, 16 * (E + 1))
            sp.wait_ge(stored[1], 16 * (TILES - EARLY_TILES))
            for b in range(NB1, NBLK):
                load(b)

            def landed(z):
                for k in range(NOB):
                    sp.wait_ge(out_done[k], 16 * ((z - k + NOB - 1) // NOB))

            further_parts(sp, lambda a, z: landed(z))
            landed(PARTS[0])
            for k in range(NROW):
                sp.wait_ge(row_in[k], 16 * ((NBLK - k + NROW - 1) // NROW))

        @block.gpsimd
        def _(pool):
            def store(n):
                pool.wait_ge(slot_ready, n + 1)
                pool.wait_ge(alpha_ready, n + 1)
                for st in GROUPS[n]:
                    for t in tiles(st):
                        pool.indirect_dma_start(scratch, bass.IndirectOffsetOnAxis(ap=slot[:, t:t + 1], axis=0),
                                                rows[:, t, :], None).then_inc(stored[n >= EARLY], 16)

            def give(b):
                pool.wait_ge(ob_ready, b + 1)
                pool.indirect_dma_start(out, bass.IndirectOffsetOnAxis(ap=rin[:, b, C_TOK:C_TOK + 1].bitcast(U32), axis=0),
                                        ob[b % NOB][:], None, bounds_check=TOKENS - 1,
                                        oob_is_err=False).then_inc(out_done[b % NOB], 16)

            for n in range(len(GROUPS) - 1):
                store(n)
            def run(a, z):
                for b in range(a, z):
                    give(b)
                    if b == POOL_LAST:
                        store(len(GROUPS) - 1)

            run(0, PARTS[0])
            pool.wait_ge(table_ready, 2)
            further_parts(pool, run)

        @block.scalar
        def _(act):
            act.dma_start(aw[:], attn_w).then_inc(aw_in, 16)
            act.dma_start(qb[:], qkv_b).then_inc(small_in, 16)
            act.dma_start(ic[:, 0:D], ident).then_inc(ident_in, 16)
            act.dma_start(pw[:], proj_w).then_inc(small_in, 16)
            act.dma_start(cf[:], const_f).then_inc(const_in, 16)
            act.dma_start(cb[:], const_b).then_inc(const_in, 16)
            act.dma_start(tokid[:], token_ids).then_inc(const_in, 16)
            act.dma_start(tc[:], table_c).then_inc(const_in, 16)
            act.dma_start(fill_sb[:], filler).then_inc(const_in, 16)

            def normalise(s, k):
                if s >= STEPS:
                    return
                if k == 0:
                    act.wait_ge(x_scalars, 1 if s < 2 else 2 if s < 4 else 3)
                    if s >= 2:
                        act.wait_ge(t_done, s - 1)
                t = ST * s + k
                act.activation(xh[s % 2][:, k, :], x_tile(t), ACT.Identity, bias=hbias[:, t:t + 1],
                               scale=rs1[:, 1, t:t + 1]).then_inc(xh_ready, 1)

            def gate(n):
                a, z = ST * GROUPS[n][0], ST * (GROUPS[n][-1] + 1)
                act.wait_ge(nlog_ready, n + 1)
                act.activation(eneg[:, a:z], nlog[:, a:z], ACT.Exp).then_inc(eneg_ready, 1)

            for k in range(ST):
                normalise(0, k)
            for s in range(STEPS + 1):
                if s < STEPS:
                    act.wait_ge(c_done, s + 1)
                    if s >= 1:
                        act.wait_ge(u_done, s)
                    act.copy(c_sb[:], ps_c[:, 0:2 * D]).then_inc(c_ready, 1)
                    normalise(s + 1, 0)
                    act.wait_ge(u_done, s + 1)
                    if s >= 1:
                        act.wait_ge(s_done, s)
                    act.copy(u_sb[:], ps_u[:, 0:2 * D]).then_inc(u_ready, 1)
                    act.wait_ge(t_done, s + 1)
                    if s >= 2:
                        act.wait_ge(o_done, s - 1)
                    act.copy(xt[s % 2][:], ps_t[:]).then_inc(xt_ready, 1)
                if s >= 1:
                    act.wait_ge(m_done, s)
                    if s >= 2:
                        act.wait_ge(g_done, s - 1)
                    act.copy(m_sb[:], ps_m[:, 0:2 * AW]).then_inc(m_ready, 1)
                if s < STEPS:
                    for k in range(1, ST):
                        normalise(s + 1, k)
                if s >= 1:
                    act.wait_ge(g_done, s)
                    if s >= 2:
                        act.wait_ge(o_done, s - 1)
                    act.copy(g_sb[:, :, 0:AW], ps_g[:, 0:2 * AW].rearrange("p (b c) -> p b c", b=2)).then_inc(g_ready, 1)
                if s < STEPS:
                    act.wait_ge(nmax_ready, s + 1)
                    if s >= 1:
                        act.wait_ge(wn_ready, s)
                    for b in range(2):
                        last = act.activation(w_sb[:, b, :], ps_s[:, b * D:(b + 1) * D], ACT.Exp, bias=nmax[:, b:b + 1],
                                              accum_out=den[:, b:b + 1])
                    last.then_inc(exp_done, 1)
                if s - 3 in GROUP_OF:
                    gate(GROUP_OF[s - 3])

            def turn(b):
                e = expert(act, b)
                weight, bias = aw[:, bass.ds(e + A_G, 1)], aw[:, bass.ds(e + A_B, 1)]
                act.wait_ge(hnt_done, b + 1)
                if b >= 2:
                    act.wait_ge(l1_done, b - 1)
                act.activation(ht[b % 2][:], ps_xt[b % 2][:, 0:P], ACT.Identity, bias=bias, scale=weight).then_inc(ht_ready, 1)
                return e

            act.wait_ge(table_ready, 1)
            act.wait_ge(w1_in, 32)

            def run(a, z):
                e_next = None
                for b in range(a - 1, z):
                    if b == NB1 - 1:
                        act.wait_ge(table_ready, 2)
                    e = e_next
                    if b == ACT_GATE:
                        gate(len(GROUPS) - 1)
                    if b + 1 < z:
                        e_next = turn(b + 1)
                    if b < a:
                        continue
                    if b >= 2:
                        act.wait_ge(base2_ready, b - 1)
                    act.activation(base[b % 2][:], rin[:, b, 0:D], ACT.Identity, bias=rin[:, b, C_SB:C_SB + 1],
                                   scale=rin[:, b, C_SA:C_SA + 1]).then_inc(base_ready, 1)
                    act.wait_ge(l1_done, b + 1)
                    if b >= 2:
                        act.wait_ge(l2_done, b - 1)
                    for c in range(act_chunks(b)):
                        last = act.activation(hid[b % 2][:, c, :], ps_ha[b % 2][:, c * P:(c + 1) * P], ACT.Relu,
                                              bias=b1_sb[:, bass.ds(e * FC + c, 1)])
                    last.then_inc(relu_a, 1)

            run(0, PARTS[0])
            further_parts(act, run)

        @block.vector
        def _(dve):
            norm, stat, route, soft, tab = [Chain(dve, c) for c in (dve_norm, dve_stat, dve_route, dve_soft, dve_table)]

            def stats1(t):
                dve.wait_ge(x_in[t // ST], 16)
                stat.mark(dve.bn_stats(bn1[:, t, :], x_tile(t)))

            def moments(bn, mom, var, a, z, k):
                norm.ready()
                if k == 0:
                    stat.ready()
                    dve.tensor_tensor(mom[:, 1, a:z], bn[:, a:z, 2], bn[:, a:z, 5], ALU.add)
                    norm.mark(dve.tensor_tensor(mom[:, 2, a:z], bn[:, a:z, 1], bn[:, a:z, 4], ALU.subtract))
                elif k == 1:
                    norm.mark(dve.scalar_tensor_tensor(out=mom[:, 3, a:z], in0=mom[:, 2, a:z], scalar=0.25,
                                                       in1=mom[:, 2, a:z], op0=ALU.mult, op1=ALU.mult))
                    norm.mark(dve.tensor_tensor(mom[:, 0, a:z], bn[:, a:z, 1], bn[:, a:z, 4], ALU.add))
                elif k == 2:
                    norm.mark(dve.scalar_tensor_tensor(out=mom[:, 1, a:z], in0=mom[:, 1, a:z], scalar=1.0 / D,
                                                       in1=mom[:, 3, a:z], op0=ALU.mult, op1=ALU.add))
                else:
                    norm.mark(dve.tensor_scalar(var[:, 0, a:z], mom[:, 1, a:z], EPS, None, ALU.add))
                    norm.mark(dve.tensor_scalar(var[:, 1, a:z], mom[:, 1, a:z], 1.0 + EPS, EPS * EPS, ALU.mult, ALU.add))

            def root(k, var, rs, nw, a, z):
                y, t = rs[:, :, a:z], nw[:, :, a:z]
                norm.ready()
                if k == 0:
                    ins = dve.tensor_scalar(y.bitcast(I32), var[:, :, a:z].bitcast(I32), -0.5, MAGIC, ALU.mult, ALU.add)
                elif k % 3 == 1:
                    ins = dve.tensor_tensor(t, y, y, ALU.mult)
                elif k % 3 == 2:
                    ins = dve.scalar_tensor_tensor(out=t, in0=t, scalar=-0.5, in1=var[:, :, a:z], op0=ALU.mult, op1=ALU.mult)
                else:
                    ins = dve.scalar_tensor_tensor(out=y, in0=t, scalar=1.5, in1=y, op0=ALU.add, op1=ALU.mult)
                norm.mark(ins)

            def scalars1(n, k):
                a, z = LN1[n]
                if k < 4:
                    moments(bn1, mom1, var1, a, z, k)
                    return
                k -= 4
                if k < ROOT:
                    root(k, var1, rs1, nw1, a, z)
                    return
                norm.ready()
                r, rho = rs1[:, 0, a:z], rs1[:, 1, a:z]
                if k == ROOT:
                    norm.mark(dve.scalar_tensor_tensor(out=nw1[:, 0, a:z], in0=mom1[:, 0, a:z], scalar=-0.5, in1=rho,
                                                       op0=ALU.mult, op1=ALU.mult))
                    norm.mark(dve.tensor_scalar(xs1[:, a:z], r, 1.0, None, ALU.add))
                elif k == ROOT + 1:
                    dve.tensor_scalar(hbias[:, a:z], nw1[:, 0, a:z], 1.0, None, ALU.add).then_inc(x_scalars, 1)
                    norm.mark(dve.tensor_tensor(nw1[:, 1, a:z], var1[:, 1, a:z], rho, ALU.mult))
                    dve.scalar_tensor_tensor(out=mr1[:, a:z], in0=mom1[:, 0, a:z], scalar=0.5, in1=r, op0=ALU.mult, op1=ALU.mult)
                elif k == ROOT + 2:
                    norm.mark(dve.tensor_tensor(rfac[:, a:z], nw1[:, 1, a:z], xs1[:, a:z], ALU.mult))

            LN1_STEPS = 4 + ROOT + 3

            dve.memset(one_d[:], 1.0 / D)
            dve.memset(acc[:, 0, :], 0.0)
            dve.wait_ge(aw_in, 16)
            norm.link(dve.tensor_tensor(nbw[:], aw[:, A_COL + 1:A_COL + 2], aw[:, A_COL:A_COL + 1], ALU.subtract))
            dve.tensor_scalar(nb_t[:], one_d[:], nbw[:], None, ALU.mult)
            dve.tensor_scalar(pb_t[:], one_d[:], aw[:, A_COL + 2:A_COL + 3], None, ALU.mult).then_inc(prep_in, 1)
            dve.tensor_copy(pt[:, 0:D], aw[:, A_P:A_P + D])
            dve.memset(done[:], 0.0)

            def fold():
                dve.wait_ge(prep_mm, 2)
                dve.scalar_tensor_tensor(out=wt[:], in0=aw[:, 0:3 * D], scalar=aw[:, A_COL:A_COL + 1], in1=bank[0][:, 0:3 * D],
                                         op0=ALU.mult, op1=ALU.add).then_inc(wt_ready, 1)
                dve.tensor_tensor(ic[:, D:AW], aw[:, A_C:A_C + E], bank[5][:, 0:E], ALU.subtract).then_inc(prep_in, 1)

            for t in range(*LN1[0]):
                stats1(t)
            for k in range(LN1_STEPS):
                scalars1(0, k)
                if k == PREP_STEP:
                    fold()
            dve.wait_ge(prep_in, 2)
            dve.wait_ge(wt_ready, 1)
            dve.tensor_scalar(wq_s[:], wt[:, 0:D], SCALE, None, ALU.mult)
            for b in range(2):
                dve.tensor_copy(g_sb[:, b, AW:OW], ic[:, D:AW])
            dve.wait_ge(prep_mm, 3)
            dve.tensor_copy(wv[:], bank[2][:, 0:D])
            for b in range(2):
                dve.tensor_scalar(pb_row[:, b, :], bank[3][0:1, 0:AW], float(D), None, ALU.mult)
            dve.tensor_copy(pt[:, D:AW], bank[4][:, 0:E]).then_inc(prep_ready, 1)
            dve.wait_ge(prep_ready, 1)
            dve.wait_ge(const_in, 16 * 5)
            dve.tensor_copy(rows[:, :, C_TOK].bitcast(I32), tokid[:])
            for t in range(*LN1[1]):
                stats1(t)
            late = range(*LN1[2])
            for k in range(LN1_BEFORE):
                stats1(late[k])
                scalars1(1, k)

            def span(n):
                return ST * GROUPS[n][0], ST * (GROUPS[n][-1] + 1)

            def choose(n, k):
                a, z = span(n)
                w = z - a
                desc = cf[:, 0:w * E].rearrange("p (t e) -> p t e", t=w)

                def wide(v):
                    return v[:, a:z].unsqueeze(2).to_broadcast([P, w, E])

                route.ready()
                if k == 0:
                    ins = dve.tensor_reduce(amax[:, a:z], aff[:, a:z, :], AX.X, ALU.max)
                elif k == 1:
                    ins = dve.tensor_tensor(hit[:, a:z, :], aff[:, a:z, :], wide(amax), ALU.is_equal)
                elif k == 2:
                    ins = dve.tensor_tensor(val[:, a:z, :], hit[:, a:z, :], desc, ALU.mult)
                elif k == 3:
                    ins = dve.tensor_reduce(first[:, a:z], val[:, a:z, :], AX.X, ALU.max)
                elif k == 4:
                    ins = dve.tensor_tensor(onehot[:, a:z, :], desc, wide(first), ALU.is_equal)
                elif k == 5:
                    ins = dve.tensor_reduce(osum[:, n, :], onehot[:, a:z, :].rearrange("p t e -> p e t"), AX.X, ALU.add)
                else:
                    if n >= 1:
                        dve.wait_ge(acc_ready, n)
                    dve.tensor_tensor(acc[:, n + 1, :], acc[:, n, :], osum[:, n, :], ALU.add).then_inc(acc_ready, 1)
                    return
                route.mark(ins)

            def residual(s, routed=None):
                dve.wait_ge(o_done, s + 1)
                both = bank_o[:, :, 0:2 * OW].rearrange("p b (j c) -> p b j c", j=2)
                a, z = ST * s, ST * (s + 1)
                cut = "p (b j) c -> p b j c"
                fac = rfac[:, a:z].rearrange("p (b j) -> p b j", b=2).unsqueeze(3).to_broadcast([P, 2, 2, E])
                n = GROUP_OF.get(s)
                route.mark(dve.tensor_tensor(aff0[:, a:z, :].rearrange(cut, b=2), both[:, :, :, AW:OW], fac, ALU.mult))
                for k in range(ST):
                    t = a + k
                    ins = dve.scalar_tensor_tensor(out=rows[:, t, 0:D], in0=x_tile(t), scalar=xs1[:, t:t + 1],
                                                   in1=bank_o[:, k // 2, (k % 2) * OW:(k % 2) * OW + D],
                                                   op0=ALU.mult, op1=ALU.add)
                    if k == 0:
                        route.ready()
                        route.mark(dve.tensor_tensor(aff[:, a:z, :].rearrange(cut, b=2), both[:, :, :, D:AW],
                                                     aff0[:, a:z, :].rearrange(cut, b=2), ALU.add))
                    elif n is not None:
                        choose(n, k - 1)
                    if s == 0:
                        scalars1(2, 4 + k)
                    if k < ST - 1 and routed is not None:
                        scalars2(routed, k)
                ins.then_inc(o_read, 1)
            def stats2(t):
                stat.mark(dve.bn_stats(bn2[:, t, :], rows[:, t, 0:D]))

            def places(n, k):
                a, z = span(n)
                w = z - a
                rank, count = (ps_rank_last, ps_cnt_last) if n == len(GROUPS) - 1 else (ps_rank, ps_cnt)
                if k == 0:
                    dve.wait_ge(rank_done, n + 1)
                    if n in ROUND_OF:
                        tab.mark(dve.tensor_copy(cnt[:, ROUND_OF[n], :], count[0:1, :]))
                    route.mark(dve.tensor_tensor(posh[:, a:z, :].rearrange("p t e -> p (t e)"), rank[:, 0:w * E],
                                                 onehot[:, a:z, :].rearrange("p t e -> p (t e)"), ALU.mult))
                elif k == 1:
                    route.ready()
                    route.mark(dve.tensor_reduce(posf[:, a:z], posh[:, a:z, :], AX.X, ALU.add))
                elif k == 2:
                    route.ready()
                    dve.tensor_copy(slot[:, a:z], posf[:, a:z]).then_inc(slot_ready, 1)

            def scalars2(n, k):
                a, z = span(n)
                if k < ROOT:
                    root(k, var2, rs2, nw2, a, z)
                    return
                norm.ready()
                r3, rh = rs2[:, 0, a:z], rs2[:, 1, a:z]
                if k == ROOT:
                    dve.scalar_tensor_tensor(out=nlog[:, a:z], in0=r3, scalar=-1.0, in1=amax[:, a:z], op0=ALU.mult,
                                             op1=ALU.mult).then_inc(nlog_ready, 1)
                    norm.mark(dve.scalar_tensor_tensor(out=msb[:, a:z], in0=mom2[:, 0, a:z], scalar=-0.5, in1=r3,
                                                       op0=ALU.mult, op1=ALU.mult))
                    dve.tensor_copy(rows[:, a:z, C_HA], rh)
                elif k == ROOT + 1:
                    dve.scalar_tensor_tensor(out=rows[:, a:z, C_HB], in0=mom2[:, 0, a:z], scalar=-0.5, in1=rh,
                                             op0=ALU.mult, op1=ALU.mult)
                    dve.tensor_scalar(rows[:, a:z, C_SA], r3, 1.0, None, ALU.add)
                    dve.tensor_tensor(rows[:, a:z, C_SB], msb[:, a:z], mr1[:, a:z], ALU.subtract)

            def gates(n, k):
                a, z = span(n)
                if k == 0:
                    dve.wait_ge(eneg_ready, n + 1)
                    soft.mark(dve.tensor_scalar(epos[:, a:z], eneg[:, a:z], 1.0, None, ALU.add))
                else:
                    soft.ready()
                    dve.reciprocal(rows[:, a:z, C_AL], epos[:, a:z]).then_inc(alpha_ready, 1)

            def table(r, k):
                a, z = (0, NB1) if r == 0 else (NB1, NBLK)
                m = z - a
                gone, move = past[:, r, 0:m, :], pastj[:, r, 0:m, :]
                tab.ready()
                if k == 0:
                    thr = tc[:, T_FULL:T_FULL + E * TILES] if r == 0 else tc[:, T_THR:T_THR + E * TILES]
                    tab.mark(dve.tensor_tensor(over[:, r], cnt[:, r, :].unsqueeze(2).to_broadcast([1, E, TILES]),
                                               thr.rearrange("p (e j) -> p e j", e=E), ALU.is_gt))
                    if r == 1:
                        tab.mark(dve.tensor_tensor(frow_f[:], cnt[:, r, :], tc[:, T_ECAP:T_ECAP + E], ALU.add))
                elif k == 1:
                    tab.mark(dve.tensor_reduce(nall[:] if r else nblk[:, 0, :], over[:, r], AX.X, ALU.add))
                    if r == 1:
                        dve.tensor_copy(fill_row[:], frow_f[:]).then_inc(fill_ready, 1)
                elif k == 2 and r == 1:
                    tab.mark(dve.tensor_tensor(nblk[:, 1, :], nall[:], done[:, 0:E], ALU.subtract))
                elif k == 3:
                    lower = tc[:, T_LOW:T_LOW + E * E].rearrange("p (e j) -> p e j", e=E)
                    tab.mark(dve.tensor_tensor(low[:, r], nblk[:, r, :].unsqueeze(1).to_broadcast([1, E, E]), lower, ALU.mult))
                    dist = gap[:] if r else tc[:, T_CAP:T_CAP + E]
                    tab.mark(dve.scalar_tensor_tensor(out=jump[:, r, :], in0=nblk[:, r, :], scalar=-float(P), in1=dist,
                                                      op0=ALU.mult, op1=ALU.add))
                elif k == 4:
                    tab.mark(dve.tensor_reduce(cum[:, r, :], low[:, r], AX.X, ALU.add))
                elif k == 5:
                    blk = tc[:, T_BLK:T_BLK + m * E].rearrange("p (b e) -> p b e", b=m)
                    tab.mark(dve.tensor_tensor(gone, blk, cum[:, r, :].unsqueeze(1).to_broadcast([1, m, E]), ALU.is_ge))
                elif k == 6:
                    tab.mark(dve.tensor_tensor(move, gone, jump[:, r, :].unsqueeze(1).to_broadcast([1, m, E]), ALU.mult))
                    tab.mark(dve.tensor_reduce(bex[:, a:z], gone, AX.X, ALU.add))
                elif k == 7:
                    tab.mark(dve.tensor_reduce(bjump[:, a:z], move, AX.X, ALU.add))
                    if r == 0:
                        tab.mark(dve.tensor_tensor(cumx[:], cum[:, 0, :], nblk[:, 0, :], ALU.subtract))
                elif k == 8:
                    tab.mark(dve.tensor_tensor(bst[:, a:z], bjump[:, a:z], ofs[:] if r else tc[:, T_B128:T_B128 + m], ALU.add))
                    if r == 0:
                        tab.mark(dve.tensor_scalar(cumx[:], cumx[:], float(NB1), None, ALU.min))
                elif k == 9:
                    dve.tensor_scalar(blk_row[:, a:z], bst[:, a:z], float(E * CAP), None, ALU.min)
                    dve.tensor_scalar(blk_exp[:, a:z], bex[:, a:z], float(E - 1), None, ALU.min).then_inc(table_ready, 1)
                    if r == 0:
                        tab.mark(dve.scalar_tensor_tensor(out=done[:, 0:E], in0=cum[:, 0, :], scalar=float(NB1),
                                                          in1=cumx[:], op0=ALU.min, op1=ALU.subtract))
                elif k == 10 and r == 0:
                    tab.mark(dve.tensor_tensor(gap[:], done[:, 1:E + 1], done[:, 0:E], ALU.subtract))
                    tab.mark(dve.scalar_tensor_tensor(out=ofs[:], in0=done[:, 0:1].to_broadcast([1, NB2]), scalar=float(P),
                                                      in1=tc[:, T_B128:T_B128 + NB2], op0=ALU.mult, op1=ALU.add))
                elif k == 11 and r == 0:
                    tab.mark(dve.scalar_tensor_tensor(out=gap[:], in0=gap[:], scalar=float(P), in1=tc[:, T_CAP:T_CAP + E],
                                                      op0=ALU.mult, op1=ALU.add))

            def routing(s, k):
                closed, older = GROUP_OF.get(s - 2), GROUP_OF.get(s - 3)
                if older is not None:
                    scalars2(older, k)
                if closed is not None and k < 7:
                    choose(closed, k)

            for s in range(STEPS + 1):
                if s == STEPS:
                    break
                for k in range(ST - 1, ROOT - 3):
                    routing(s, k)
                    if s == 2:
                        scalars1(2, 5 + k)
                dve.wait_ge(s_done, s + 1)
                dve.tensor_reduce(nmax[:], ps_s[:, 0:2 * D].rearrange("p (b k) -> p b k", b=2), AX.X, ALU.max,
                                  negate=True).then_inc(nmax_ready, 1)
                for k in range(ST):
                    if s >= 2:
                        if k == 0:
                            dve.wait_ge(o_read, s - 1)
                        stats2(ST * (s - 2) + k)
                    routing(s, ROOT - 3 + k)
                    if s == 1:
                        scalars1(2, k)
                    if s == 2:
                        scalars1(2, ROOT + 2 + k)
                dve.wait_ge(exp_done, s + 1)
                soft.link(dve.reciprocal(rden[:], den[:]))
                if s >= 1:
                    dve.wait_ge(m_done, s)
                dve.tensor_tensor(wn_sb[:], w_sb[:], rden[:].unsqueeze(2).to_broadcast([P, 2, D]),
                                  ALU.mult).then_inc(wn_ready, 1)
                if s == 0:
                    for k in range(LN1_BEFORE, LN1_STEPS):
                        if k < len(late):
                            stats1(late[k])
                        scalars1(1, k)
                routing(s, ROOT + 1)
                if s == 2:
                    scalars1(2, LN1_STEPS - 1)
                older = GROUP_OF.get(s - 3)
                n = GROUP_OF.get(s - 2)
                for k in range(4):
                    if older is not None and k < 2:
                        gates(older, k)
                    if n is not None:
                        moments(bn2, mom2, var2, *span(n), k)
                        places(n, k)
                if s >= 1:
                    residual(s - 1, n)

            def whiten(b):
                dve.wait_ge(row_in[b % NROW], 16 * (b // NROW + 1))
                if b >= 2:
                    dve.wait_ge(hnt_done, b - 1)
                dve.tensor_scalar(hn[b % 2][:], rin[:, b, 0:D], rin[:, b, C_HA:C_HA + 1], rin[:, b, C_HB:C_HB + 1],
                                  ALU.mult, ALU.add).then_inc(hn_ready, 1)

            def fetch_w1(b, e):
                src = w1_sb[:, bass.ds(e * F, F)]
                if b >= 2:
                    dve.wait_ge(l1_done, b - 1)
                dve.tensor_copy(w1_now[b % 2][:], src).then_inc(w1_ready, 1)

            n, older = len(GROUPS) - 1, GROUP_OF.get(STEPS - 3)
            for k in range(10):
                routing(STEPS, ST - 1 + k)
                table(0, k)
            for t in tiles(STEPS - 2):
                stats2(t)
            dve.wait_ge(w1_in, 32)
            dve.wait_ge(w2_in, 32)
            dve.wait_ge(table_ready, 1)
            e_next, e_after = expert(dve, 0), expert(dve, 1)
            residual(STEPS - 1)
            for k in range(ST - 1, 7):
                choose(n, k)
                if k < ST + 1:
                    table(0, 10 + k - (ST - 1))
            if older is not None:
                gates(older, 0)
            fetch_w1(0, e_next)
            if older is not None:
                gates(older, 1)
            for t in tiles(STEPS - 1):
                stats2(t)
            whiten(0)
            whiten(1)

            def tail(k):
                if k < 4:
                    moments(bn2, mom2, var2, *span(n), k)
                    places(n, k)
                    return
                k -= 4
                if k < ROOT + 2:
                    scalars2(n, k)
                    if k < 2:
                        table(1, k)
                elif k < ROOT + 4:
                    gates(n, k - ROOT - 2)
                elif k < ROOT + 12:
                    table(1, 2 + k - ROOT - 4)

            def tail_part(b, k):
                if b < TAIL_FULL:
                    tail(4 * b + k)
                elif b < NB1 - 2 and k % 2 == 1:
                    tail(4 * TAIL_FULL + 2 * (b - TAIL_FULL) + k // 2)

            def run(a, z):
                e_next, e_after = expert(dve, a), expert(dve, a + 1)
                fetch_w1(a, e_next)
                whiten(a)
                whiten(a + 1)
                blocks(a, z, e_next, e_after)

            def blocks(a, z, e_next, e_after):
                for b in range(a, z + 1):
                    if b < z:
                        e, e_next = e_next, e_after
                        if b + 1 < z:
                            fetch_w1(b + 1, e_next)
                        if b + 2 < z:
                            whiten(b + 2)
                        if b + 2 == NB1:
                            dve.wait_ge(table_ready, 2)
                        if b + 2 < z:
                            e_after = expert(dve, b + 2)
                        biases = [b1_sb[:, bass.ds(e * FC + c, 1)] for c in range(act_chunks(b), FC)]
                        add = b2_sb[:, bass.ds(e * D, D)]
                        tail_part(b, 0)
                        dve.wait_ge(l1_done, b + 1)
                        if b >= 2:
                            dve.wait_ge(l2_done, b - 1)
                        for c in range(act_chunks(b), FC):
                            k = c - act_chunks(b)
                            last = dve.tensor_scalar(hid[b % 2][:, c, :], ps_hb[b % 2][:, k * P:(k + 1) * P],
                                                     biases[k], 0.0, ALU.add, ALU.max)
                        last.then_inc(relu_b, 1)
                        tail_part(b, 1)
                        dve.wait_ge(base_ready, b + 1)
                        if b >= 2:
                            dve.wait_ge(ob_ready, b - 1)
                        dve.scalar_tensor_tensor(out=base2[b % 2][:], in0=add, scalar=rin[:, b, C_AL:C_AL + 1],
                                                 in1=base[b % 2][:], op0=ALU.mult, op1=ALU.add).then_inc(base2_ready, 1)
                        tail_part(b, 2)
                    if b > a:
                        q = b - 1
                        dve.wait_ge(l2_done, q + 1)
                        dve.wait_ge(base2_ready, q + 1)
                        if q >= NOB:
                            dve.wait_ge(out_done[q % NOB], 16 * (q // NOB))
                        dve.scalar_tensor_tensor(out=ob[q % NOB][:], in0=ps_y[q % 2][:, 0:D], scalar=rin[:, q, C_AL:C_AL + 1],
                                                 in1=base2[q % 2][:], op0=ALU.mult, op1=ALU.add).then_inc(ob_ready, 1)
                    tail_part(b, 3)

            blocks(0, PARTS[0], e_next, e_after)
            further_parts(dve, run)

        @block.tensor
        def _(pe):
            def mm(out, lhs, rhs, start=True, stop=True):
                return pe.matmul(out, lhs, rhs, start=start, stop=stop)

            pe.wait_ge(prep_in, 1)
            pe.wait_ge(small_in, 32)
            mm(bank[0][:, 0:3 * D], nb_t[:], aw[:, 0:3 * D], stop=False)
            mm(bank[0][:, 0:3 * D], one_d[0:1, :], qb[:], start=False).then_inc(prep_mm, 1)
            mm(bank[5][:, 0:E], one_d[:], aw[:, A_C:A_C + E]).then_inc(prep_mm, 1)
            pe.wait_ge(ident_in, 16)
            pe.wait_ge(prep_in, 2)
            pe.transpose(bank[2][:, 0:D], wt[:, 2 * D:3 * D], idt)
            mm(bank[3][:, 0:AW], pb_t[:], ic[:])
            mm(bank[4][:, 0:E], pw[:], ic[:, D:AW]).then_inc(prep_mm, 1)

            def ranks(n, s):
                a, z = ST * GROUPS[n][0], ST * (GROUPS[n][-1] + 1)
                w = z - a
                oh = onehot[:, a:z, :].rearrange("p t e -> p (t e)")
                if n < len(GROUPS) - 1:
                    rank, count = ps_rank, ps_cnt
                    pe.wait_ge(g_ready, s)
                else:
                    rank, count = ps_rank_last, ps_cnt_last
                    pe.wait_ge(o_read, STEPS)
                pe.wait_ge(acc_ready, n + 1)
                if n in ROUND_OF:
                    mm(count, ones_b, acc[:, n + 1, :])
                mm(rank[:, 0:w * E], ones_b[0:1, :], begins[:, 0:w * E], stop=False)
                mm(rank[:, 0:w * E], tri, oh, start=False, stop=False)
                for t in range(1, w):
                    mm(rank[:, t * E:w * E], ones_b, oh[:, 0:(w - t) * E], start=False, stop=False)
                mm(rank[:, 0:w * E], ones_b, acc[:, n, :].unsqueeze(1).to_broadcast([P, w, E]),
                   start=False).then_inc(rank_done, 1)

            def products(s):
                if s >= 1:
                    pe.wait_ge(c_ready, s)
                for b in range(2):
                    for j in range(2):
                        h = xh[s % 2][:, 2 * b + j, :]
                        pe.wait_ge(xh_ready, ST * s + 2 * b + j + 1)
                        last = mm(ps_c[:, b * D:(b + 1) * D], h, h, start=(j == 0), stop=(j == 1))
                last.then_inc(c_done, 1)

            products(0)
            pe.wait_ge(prep_ready, 1)
            pe.wait_ge(const_in, 16 * 5)
            for s in range(STEPS + 1):
                if s < STEPS:
                    pe.wait_ge(c_ready, s + 1)
                    if s >= 1:
                        pe.wait_ge(u_ready, s)
                    for b in range(2):
                        last = mm(ps_u[:, b * D:(b + 1) * D], c_sb[:, b * D:(b + 1) * D], wk_t)
                    last.then_inc(u_done, 1)
                    if s >= 1:
                        pe.wait_ge(xt_ready, s)
                    for k in range(ST):
                        last = pe.transpose(ps_t[:, k * P:(k + 1) * P], xh[s % 2][:, k, :], idt)
                    last.then_inc(t_done, 1)
                if s >= 1:
                    pe.wait_ge(wn_ready, s)
                    if s >= 2:
                        pe.wait_ge(m_ready, s - 1)
                    for b in range(2):
                        last = mm(ps_m[:, b * AW:(b + 1) * AW], wn_sb[:, b, :], pt[:])
                    last.then_inc(m_done, 1)
                if s < STEPS:
                    pe.wait_ge(u_ready, s + 1)
                    if s >= 1:
                        pe.wait_ge(exp_done, s)
                    mm(ps_s[:, 0:2 * D], wq_s[:], u_sb[:]).then_inc(s_done, 1)
                if s >= 1:
                    if s >= 2:
                        pe.wait_ge(g_ready, s - 1)
                    if s - 3 in GROUP_OF:
                        pe.wait_ge(slot_ready, GROUP_OF[s - 3] + 1)
                    mm(ps_g[:, 0:2 * AW], one_d[0:1, :], pb_row[:].rearrange("p b c -> p (b c)"), stop=False)
                    pe.wait_ge(m_ready, s)
                    mm(ps_g[:, 0:2 * AW], wv[:], m_sb[:], start=False).then_inc(g_done, 1)
                if s + 1 < STEPS:
                    products(s + 1)
                if s - 2 in GROUP_OF and s < STEPS:
                    ranks(GROUP_OF[s - 2], s)
                if s >= 1:
                    pe.wait_ge(g_ready, s)
                    pe.wait_ge(xt_ready, s)
                    if s >= 2:
                        pe.wait_ge(o_read, s - 1)
                    for k in range(ST):
                        last = mm(bank_o[:, k // 2, (k % 2) * OW:(k % 2 + 1) * OW], xt[(s - 1) % 2][:, k * P:(k + 1) * P],
                                  g_sb[:, k // 2, :])
                    last.then_inc(o_done, 1)

            def turn(b):
                pe.wait_ge(hn_ready, b + 1)
                if b >= 2:
                    pe.wait_ge(ht_ready, b - 1)
                pe.transpose(ps_xt[b % 2][:, 0:P], hn[b % 2][:], idt).then_inc(hnt_done, 1)

            ranks(len(GROUPS) - 1, STEPS)
            pe.wait_ge(table_ready, 1)
            pe.wait_ge(w2_in, 32)

            def run(a, z):
                turn(a)
                e = None
                for b in range(a, z + 1):
                    e_last = e
                    if b < z:
                        e = expert(pe, b)
                        if b + 1 < z:
                            turn(b + 1)
                        pe.wait_ge(ht_ready, b + 1)
                        pe.wait_ge(w1_ready, b + 1)
                        if b >= 2:
                            pe.wait_ge(relu_a, b - 1)
                            pe.wait_ge(relu_b, b - 1)
                        for c in range(FC):
                            half, k = (ps_ha, c) if c < act_chunks(b) else (ps_hb, c - act_chunks(b))
                            last = mm(half[b % 2][:, k * P:(k + 1) * P], w1_now[b % 2][:, c * P:(c + 1) * P], ht[b % 2][:])
                        last.then_inc(l1_done, 1)
                        if b == NB1 - 1:
                            pe.wait_ge(table_ready, 2)
                    if b > a:
                        q = b - 1
                        second = [w2_sb[:, bass.ds((e_last * FC + c) * D, D)] for c in range(FC)]
                        pe.wait_ge(relu_a, q + 1)
                        pe.wait_ge(relu_b, q + 1)
                        if q == 1:
                            pe.wait_ge(slot_ready, len(GROUPS))
                        if q >= 2:
                            pe.wait_ge(ob_ready, q - 1)
                        for c in range(FC):
                            last = mm(ps_y[q % 2][:, 0:D], hid[q % 2][:, c, :], second[c], start=(c == 0), stop=(c == FC - 1))
                        last.then_inc(l2_done, 1)

            run(0, PARTS[0])
            further_parts(pe, run)


def kernel(L0_attn_x, L0_attn_norm_w, L0_attn_norm_b, L0_attn_qkv_w, L0_attn_qkv_b, L0_attn_proj_w, L0_attn_proj_b,
           L0_ffn_centroids, L0_ffn_ln_g, L0_ffn_ln_b, L0_ffn_w1, L0_ffn_b1, L0_ffn_w2, L0_ffn_b2):
    import concourse.bacc as bacc
    from concourse.bass_utils import run_bass_kernel_spmd

    f = np.float32
    attn_w = np.concatenate(
        [L0_attn_qkv_w.T, L0_attn_proj_w.T, L0_ffn_centroids.T, L0_ffn_ln_g.T, L0_ffn_ln_b.T,
         L0_attn_norm_w[:, None], L0_attn_norm_b[:, None], L0_attn_proj_b[:, None]], axis=1)
    arrays = {
        "x": np.reshape(L0_attn_x, (B, P, 2, D)).transpose(1, 0, 2, 3).reshape(P, B, 2 * D),
        "attn_w": attn_w,
        "proj_w": L0_attn_proj_w,
        "qkv_b": L0_attn_qkv_b[None, :],
        "w1": L0_ffn_w1.transpose(2, 0, 1).reshape(D, E * F),
        "w2": L0_ffn_w2.reshape(E, D, FC, P).transpose(3, 0, 2, 1).reshape(P, E * FC * D),
        "b1": L0_ffn_b1.reshape(E * FC, P).T,
        "b2": L0_ffn_b2.reshape(E * D),
    }
    import ml_dtypes
    eight = np.arange(E)
    const_f = np.zeros((P, K_END), f)
    const_f[:] = np.tile(E - eight, WMAX)
    p, m = np.arange(P)[:, None], np.arange(P)[None, :]
    begins = np.tile(eight * CAP, (P, WMAX))
    const_b = np.concatenate([p < m, np.ones((P, P)), begins], axis=1).astype(ml_dtypes.bfloat16)
    assert (const_b[:, 2 * P:].astype(f) == begins).all()
    tile = np.arange(TILES)[None, :]
    filler = np.zeros((P, RW), np.int32)
    filler[:, C_TOK] = NO_TOKEN
    table = np.zeros((1, T_END), f)
    table[0, T_BLK:T_BLK + NBLK * E] = np.repeat(np.arange(NBLK), E)
    table[0, T_THR:T_THR + E * TILES] = np.tile(np.arange(TILES) * P, E)
    table[0, T_FULL:T_FULL + E * TILES] = np.tile(np.arange(TILES) * P + P - 1, E)
    table[0, T_LOW:T_LOW + E * E] = (eight[None, :] <= eight[:, None]).reshape(-1)
    table[0, T_B128:T_B128 + NBLK] = np.arange(NBLK) * P
    table[0, T_ECAP:T_ECAP + E] = eight * CAP
    table[0, T_CAP:T_CAP + E] = CAP
    arrays.update({
        "const_f": const_f, "const_b": const_b, "ident": np.eye(P, dtype=f),
        "token_ids": (tile // 2 * L + 2 * p + tile % 2).astype(np.int32),
        "table_c": table, "filler": filler.view(f),
    })
    nc = bacc.Bacc("TRN2", target_bir_lowering=False, num_devices=1)
    feed, args = {}, []
    for name, a in arrays.items():
        a = np.ascontiguousarray(a)
        feed[f"in_{name}"] = a
        args.append(nc.dram_tensor(f"in_{name}", a.shape, mybir.dt.from_np(a.dtype), kind="ExternalInput").ap())
    args.append(nc.dram_tensor("out", (TOKENS, D), F32, kind="ExternalOutput").ap())
    build(nc, *args)
    r = run_bass_kernel_spmd(nc, [feed], core_ids=[0])
    return np.reshape(r.results[0]["out"], (B, L, D))
```
